# Optimizing a Trainium2 kernel written in Bass

```python
import numpy as np
import jax
import jax.numpy as jnp

def _softmax(x, axis=-1):
    return jax.nn.softmax(x, axis=axis)

def _gelu(x):
    return jax.nn.gelu(x, approximate=True)

def _silu(x):
    return jax.nn.silu(x)

def _sigmoid(x):
    return jax.nn.sigmoid(x)

def _layernorm(x, axis=-1, eps=1e-05):
    m = jnp.mean(x, axis=axis, keepdims=True)
    v = jnp.var(x, axis=axis, keepdims=True)
    return (x - m) / jnp.sqrt(v + eps)

def _scatter_add(tgt, idx, src, axis=0):
    return tgt.at[idx].add(src)

def _segment_sum(src, seg, n):
    return jax.ops.segment_sum(src, seg, n)
kernel_name = 'mk_cond_resid_d4_seqx_r4_f94998'

def setup_inputs(seed: int=0):
    np.random.seed(seed)
    _w = jnp.asarray

    def _rec_inputs():
        import jax
        import jax.numpy as jnp
        _rk = jax.random.key(seed)
        x = 7.22e-05 + 1 * jax.random.normal(jax.random.fold_in(_rk, 1), (16, 256, 256), jnp.float32)
        _lenS = 256 - jax.random.randint(jax.random.fold_in(_rk, 7), (16,), 0, max(1, 256 // 4) + 1, jnp.int32)
        _lenS2 = 256 - jax.random.randint(jax.random.fold_in(_rk, 8), (16,), 0, max(1, 256 // 4) + 1, jnp.int32)
        cond_512 = 0.0061147 + 1.02565 * jax.random.normal(jax.random.fold_in(_rk, 11), (16, 128), jnp.float32)
        return (x, cond_512)
    x, cond_512 = _rec_inputs()

    def _L0_cond_setup():
        import jax, jax.numpy as jnp
        import numpy as np
        import math
        HEAD_NUM = 16
        EPS = 1e-08

        def modulated_linear(x, s, aff_w, aff_b, w, b):
            style = s @ aff_w.T + aff_b
            w_mod = w[None, :, :] * style[:, None, :]
            demod = jax.lax.rsqrt(jnp.sum(w_mod * w_mod, axis=2) + EPS)
            w_mod = w_mod * demod[:, :, None]
            return jnp.einsum('bni,boi->bno', x, w_mod) + b
        key = jax.random.key(seed)
        ks = jax.random.split(key, 6)
        B, N, F, S = (8, 256, 256, 128)
        return {'x': jax.random.normal(ks[0], (B, N, F), dtype=jnp.float32), 's': jax.random.normal(ks[1], (B, S), dtype=jnp.float32), 'k_aff_w': jax.random.normal(ks[2], (F, S), dtype=jnp.float32) * 0.02, 'k_aff_b': jnp.ones((F,), dtype=jnp.float32), 'k_w': jax.random.normal(ks[3], (F, F), dtype=jnp.float32) * 0.02, 'k_b': jnp.zeros((F,), dtype=jnp.float32), 'o_aff_w': jax.random.normal(ks[4], (F, S), dtype=jnp.float32) * 0.02, 'o_aff_b': jnp.ones((F,), dtype=jnp.float32), 'o_w': jax.random.normal(ks[5], (F, F), dtype=jnp.float32) * 0.02, 'o_b': jnp.zeros((F,), dtype=jnp.float32)}
    _L0_cond_all = _L0_cond_setup()
    _L0_cond_in = {k: v for k, v in _L0_cond_all.items() if k in ('k_aff_w', 'k_aff_b', 'k_w', 'k_b', 'o_aff_w', 'o_aff_b', 'o_w', 'o_b')}
    del _L0_cond_all

    def _L1_cond_setup():
        import jax, jax.numpy as jnp
        import numpy as np
        W_DIM = 128
        CLAMP = 256.0
        key = jax.random.key(seed)
        ks = jax.random.split(key, 6)
        B, L, C = (8, 2048, 256)
        return {'x': jax.random.normal(ks[0], (B, L, C), dtype=jnp.float32), 'w': jax.random.normal(ks[1], (B, W_DIM), dtype=jnp.float32), 'weight': jax.random.normal(ks[2], (C, C), dtype=jnp.float32), 'bias': jax.random.normal(ks[3], (C,), dtype=jnp.float32), 'affine_w': jax.random.normal(ks[4], (C, W_DIM), dtype=jnp.float32), 'affine_b': jnp.ones((C,), dtype=jnp.float32)}
    _L1_cond_all = _L1_cond_setup()
    _L1_cond_in = {k: v for k, v in _L1_cond_all.items() if k in ('weight', 'bias', 'affine_w', 'affine_b')}
    del _L1_cond_all

    def _L2_cond_setup():
        import jax, jax.numpy as jnp
        import numpy as np
        B, S, D, H, C = (8, 1024, 256, 64, 128)
        INIT_RANGE = 0.01
        key = jax.random.key(seed)
        ks = jax.random.split(key, 6)
        return {'hidden_states': jax.random.normal(ks[0], (B, S, D), dtype=jnp.float32), 'conditions': jax.random.normal(ks[1], (B, C), dtype=jnp.float32), 'down_project': jax.random.normal(ks[2], (D, H), dtype=jnp.float32) * INIT_RANGE, 'down_gamma': jax.random.normal(ks[3], (C, H), dtype=jnp.float32), 'down_beta': jnp.zeros((C, H), dtype=jnp.float32), 'up_project': jax.random.normal(ks[4], (H, D), dtype=jnp.float32) * INIT_RANGE, 'up_gamma': jax.random.normal(ks[5], (C, D), dtype=jnp.float32), 'up_beta': jnp.zeros((C, D), dtype=jnp.float32)}
    _L2_cond_all = _L2_cond_setup()
    _L2_cond_in = {k: v for k, v in _L2_cond_all.items() if k in ('down_project', 'down_gamma', 'down_beta', 'up_project', 'up_gamma', 'up_beta')}
    del _L2_cond_all

    def _L3_cond_setup():
        import jax, jax.numpy as jnp
        import numpy as np
        IN_DIM = 256
        OUT_DIM = 256
        MU_DIM = 128
        K = 30
        key = jax.random.key(seed)
        k1, k2, k3, k4, k5 = jax.random.split(key, 5)
        B, S = (16, 512)
        x = jax.random.normal(k1, (B, S, IN_DIM), dtype=jnp.float32)
        mu = jax.random.normal(k2, (B, MU_DIM), dtype=jnp.float32)
        W_dec = jax.random.normal(k3, (MU_DIM, (IN_DIM + 1) * K), dtype=jnp.float32) / np.sqrt(MU_DIM)
        b_dec = jax.random.normal(k4, ((IN_DIM + 1) * K,), dtype=jnp.float32) * 0.01
        V = jax.random.normal(k5, (K, OUT_DIM), dtype=jnp.float32) / np.sqrt(K)
        return {'x': x, 'mu': mu, 'W_dec': W_dec, 'b_dec': b_dec, 'V': V}
    _L3_cond_all = _L3_cond_setup()
    _L3_cond_in = {k: v for k, v in _L3_cond_all.items() if k in ('W_dec', 'b_dec', 'V')}
    del _L3_cond_all
    return {'x': x, 'cond_512': cond_512, 'L0_cond_k_aff_w': _L0_cond_in['k_aff_w'], 'L0_cond_k_aff_b': _L0_cond_in['k_aff_b'], 'L0_cond_k_w': _L0_cond_in['k_w'], 'L0_cond_k_b': _L0_cond_in['k_b'], 'L0_cond_o_aff_w': _L0_cond_in['o_aff_w'], 'L0_cond_o_aff_b': _L0_cond_in['o_aff_b'], 'L0_cond_o_w': _L0_cond_in['o_w'], 'L0_cond_o_b': _L0_cond_in['o_b'], 'L1_cond_weight': _L1_cond_in['weight'], 'L1_cond_bias': _L1_cond_in['bias'], 'L1_cond_affine_w': _L1_cond_in['affine_w'], 'L1_cond_affine_b': _L1_cond_in['affine_b'], 'L2_cond_down_project': _L2_cond_in['down_project'], 'L2_cond_down_gamma': _L2_cond_in['down_gamma'], 'L2_cond_down_beta': _L2_cond_in['down_beta'], 'L2_cond_up_project': _L2_cond_in['up_project'], 'L2_cond_up_gamma': _L2_cond_in['up_gamma'], 'L2_cond_up_beta': _L2_cond_in['up_beta'], 'L3_cond_W_dec': _L3_cond_in['W_dec'], 'L3_cond_b_dec': _L3_cond_in['b_dec'], 'L3_cond_V': _L3_cond_in['V']}

def reference(x, cond_512, L0_cond_k_aff_w, L0_cond_k_aff_b, L0_cond_k_w, L0_cond_k_b, L0_cond_o_aff_w, L0_cond_o_aff_b, L0_cond_o_w, L0_cond_o_b, L1_cond_weight, L1_cond_bias, L1_cond_affine_w, L1_cond_affine_b, L2_cond_down_project, L2_cond_down_gamma, L2_cond_down_beta, L2_cond_up_project, L2_cond_up_gamma, L2_cond_up_beta, L3_cond_W_dec, L3_cond_b_dec, L3_cond_V):
    import jax
    import jax.numpy as jnp

    def _L0_cond_ref(x, s, k_aff_w, k_aff_b, k_w, k_b, o_aff_w, o_aff_b, o_w, o_b):
        import jax, jax.numpy as jnp
        import numpy as np
        import math
        HEAD_NUM = 16
        EPS = 1e-08

        def modulated_linear(x, s, aff_w, aff_b, w, b):
            style = s @ aff_w.T + aff_b
            w_mod = w[None, :, :] * style[:, None, :]
            demod = jax.lax.rsqrt(jnp.sum(w_mod * w_mod, axis=2) + EPS)
            w_mod = w_mod * demod[:, :, None]
            return jnp.einsum('bni,boi->bno', x, w_mod) + b
        B, N, F = x.shape
        H = HEAD_NUM
        D = F // H
        kx = modulated_linear(x, s, k_aff_w, k_aff_b, k_w, k_b)
        kx = kx.reshape(B, N, H, D)
        q = k = v = kx
        scores = jnp.einsum('bnhd,bnjd->bnhj', q, k) / math.sqrt(D)
        A = jax.nn.softmax(scores, axis=-1)
        out = jnp.einsum('bnhj,bnjd->bnhd', A, v).reshape(B, N, F)
        out = modulated_linear(out, s, o_aff_w, o_aff_b, o_w, o_b)
        return out

    def _L1_cond_ref(x, w, weight, bias, affine_w, affine_b):
        import jax, jax.numpy as jnp
        import numpy as np
        W_DIM = 128
        CLAMP = 256.0
        B, L, C = x.shape
        gain = 1.0 / np.sqrt(W_DIM).astype(np.float32)
        styles = w @ (affine_w * gain).T + affine_b
        ws = weight[None, :, :] * styles[:, None, :]
        dcoefs = jax.lax.rsqrt(jnp.sum(ws * ws, axis=2) + 1e-08)
        xm = x * styles[:, None, :]
        y = jnp.einsum('blc,oc->blo', xm, weight)
        y = y * dcoefs[:, None, :]
        y = jnp.clip(y + bias, -CLAMP, CLAMP)
        return y

    def _L2_cond_ref(hidden_states, conditions, down_project, down_gamma, down_beta, up_project, up_gamma, up_beta):
        import jax, jax.numpy as jnp
        import numpy as np
        B, S, D, H, C = (8, 1024, 256, 64, 128)
        INIT_RANGE = 0.01
        dg = conditions @ down_gamma
        db = conditions @ down_beta
        ug = conditions @ up_gamma
        ub = conditions @ up_beta
        w_down = down_project[None, :, :] * dg[:, None, :] + db[:, None, :]
        down = jnp.einsum('bsd,bdh->bsh', hidden_states, w_down)
        act = jax.nn.relu(down)
        w_up = up_project[None, :, :] * ug[:, None, :] + ub[:, None, :]
        up = jnp.einsum('bsh,bhd->bsd', act, w_up)
        return up + hidden_states

    def _L3_cond_ref(x, mu, W_dec, b_dec, V):
        import jax, jax.numpy as jnp
        import numpy as np
        IN_DIM = 256
        OUT_DIM = 256
        MU_DIM = 128
        K = 30
        B = mu.shape[0]
        U = (mu @ W_dec + b_dec).reshape(B, IN_DIM + 1, K)
        param = jnp.einsum('bik,kj->bij', U, V)
        weight = param[:, :-1, :]
        bias = param[:, -1, :]
        out = jnp.einsum('bsd,bde->bse', x, weight)
        out = out + bias[:, None, :]
        return out
    x = x + _L0_cond_ref(x, cond_512, L0_cond_k_aff_w, L0_cond_k_aff_b, L0_cond_k_w, L0_cond_k_b, L0_cond_o_aff_w, L0_cond_o_aff_b, L0_cond_o_w, L0_cond_o_b)
    x = x + _L1_cond_ref(x, cond_512, L1_cond_weight, L1_cond_bias, L1_cond_affine_w, L1_cond_affine_b)
    x = x + _L2_cond_ref(x, cond_512, L2_cond_down_project, L2_cond_down_gamma, L2_cond_down_beta, L2_cond_up_project, L2_cond_up_gamma, L2_cond_up_beta)
    x = x + _L3_cond_ref(x, cond_512, L3_cond_W_dec, L3_cond_b_dec, L3_cond_V)
    return x

_drawn_inputs = setup_inputs


def setup_inputs(seed=0):
    import zlib

    import numpy as np

    out = dict(_drawn_inputs(seed))
    spreads = {'L0_cond_k_aff_b': (1.0, 0.2),
     'L0_cond_k_b': (0.0, 0.622),
     'L0_cond_o_aff_b': (1.0, 0.2),
     'L0_cond_o_b': (0.0, 0.577),
     'L1_cond_affine_b': (1.0, 0.6),
     'L2_cond_down_beta': (0.0, 0.1),
     'L2_cond_up_beta': (0.0, 0.1)}
    factors = {'L1_cond_bias': 5.753,
     'L2_cond_down_gamma': 2.704,
     'L2_cond_up_project': 2.93,
     'L2_cond_up_gamma': 2.745,
     'L3_cond_b_dec': 6.046}
    for name, (base, spread) in spreads.items():
        noise = np.random.default_rng([zlib.crc32(name.encode()), seed]).standard_normal(out[name].shape)
        drawn = base * np.exp(spread * noise) if base else spread * noise
        out[name] = jnp.asarray(drawn.astype(out[name].dtype))
    for name, factor in factors.items():
        out[name] = (out[name] * factor).astype(out[name].dtype)
    return out
```

```python
from collections import namedtuple
from contextlib import ExitStack

import concourse.bass as bass
from concourse import mybir

ALU = mybir.AluOpType
ACT = mybir.ActivationFunctionType
AX_X = mybir.AxisListType.X
F32 = mybir.dt.float32
BF16 = mybir.dt.bfloat16

P = 128
LAYERS = 3
NEG = -1e30
EPS = 1e-8
CLAMP = 256.0

LEFT_PARTS = "hhmhml"
RIGHT_PARTS = "hmhlmh"

Step = namedtuple("Step", "i par uses")


def following(s):
    return Step(s.i + 1, 1 - s.par, s.uses + s.par)


def preceding(s):
    return Step(s.i - 1, 1 - s.par, s.uses - (1 - s.par))


def wait(eng, sem, count):
    if isinstance(count, int) and count <= 0:
        return
    eng.wait_ge(sem, count)


def held(eng, *values):
    return [v if isinstance(v, int) else eng.snap(v) for v in values]


def cond_resid_kernel(nc, x, cond, ka_w, ka_b, k_w, k_b, oa_w, oa_b, o_w, o_b, w1, b1, la_w, la_b,
                      down, dgamma, dbeta, up, ugamma, ubeta, w_dec, b_dec, v_mat, out):
    B, N, F = x.shape
    S = cond.shape[1]
    H = 16
    D = F // H
    KC = F // P
    RANK = v_mat.shape[0]
    HID = down.shape[1]
    NB = 2
    T = NB * N
    STEPS = B // NB
    Q = T // P
    CH = 4
    XT = 8
    G = T // XT
    GC = G // CH
    GAIN = 1.0 / float(S) ** 0.5
    NDEC = w_dec.shape[1]
    UCH = 16
    assert (B, N, F, S, D, KC, XT * H) == (16, 256, 256, P, 16, 2, P) and NDEC == (F + 1) * RANK

    x_rows = x.rearrange("b n f -> (b n) f")
    out_rows = out.rearrange("b n f -> (b n) f")
    rows_dram = nc.dram_tensor("rows_dram", (B, 2 * HID + 2 * F), F32, kind="Internal").ap()
    u_dram = nc.dram_tensor("u_dram", (B, UCH * 512), F32, kind="Internal").ap()
    keys_dram = nc.dram_tensor("keys_dram", (2, D, H, T), F32, kind="Internal").ap()

    with ExitStack() as ctx:
        def sb(name, shape, dt=F32):
            return ctx.enter_context(nc.sbuf_tensor(name, shape, dt))

        def sem(name):
            return ctx.enter_context(nc.semaphore(name))

        ident = sb("ident", [P, P])
        cond_t = sb("cond_t", [P, 32])
        table_a = sb("table_a", [P, STEPS, 8])
        table_c = sb("table_c", [P, STEPS, 17])
        cur_a = sb("cur_a", [P, 8])
        cur_c = sb("cur_c", [P, 17])
        w_t = sb("w_t", [P, LAYERS, KC, F])
        down_sb = sb("down_sb", [P, KC, HID])
        up_pad = sb("up_pad", [P, NB, F])
        v_pad = sb("v_pad", [P, NB, F])
        u_all = sb("u_all", [P, B, KC, RANK])
        biases = sb("biases", [P, 9, KC])
        eps_t = sb("eps_t", [P, 96])
        b_dec_t = sb("b_dec_t", [P, KC, RANK])
        ybias = sb("ybias", [P, STEPS])
        b_dec_c = sb("b_dec_c", [P, 1])
        mask = sb("mask", [P, 2, T], BF16)
        style = sb("style", [P, 6, B])
        style2 = sb("style2", [P, 6, B])
        x_in = sb("x_in", [P, 2, Q, F])
        x_t = sb("x_t", [P, 2, KC, T])
        keys = sb("keys", [P, KC, T])
        rest = sb("rest", [P, KC, T])
        part = {c: sb(f"part_{c}", [P, KC, T], BF16) for c in "hml"}
        gram = sb("gram", [P, 2, 2, H, T], BF16)
        keys_v = sb("keys_v", [P, 2, D, G])
        z = sb("z", [P, 2, GC, 32])
        z_t = sb("z_t", [P, 2, GC, 32])
        diag = sb("diag", [P, 2, GC, P])
        row_max = sb("row_max", [P, GC])
        row_sum = sb("row_sum", [P, GC])
        row_inv = sb("row_inv", [P, 2, GC])
        o_rows = sb("o_rows", [P, H, XT, GC])
        o_t = sb("o_t", [P, KC, CH, XT, GC])
        y = sb("y", [P, KC, T])
        x1 = sb("x1", [P, KC, T])
        x2 = sb("x2", [P, KC, T])
        x3 = sb("x3", [P, KC, T])
        act2 = sb("act2", [P, N])
        y3 = sb("y3", [P, N])
        out_sb = sb("out_sb", [P, Q, F])
        w_mod = [sb(f"w_mod{n}", [P, NB, KC, F]) for n in range(LAYERS)]
        down_row = sb("down_row", [P, NB, 2, HID])
        up_row = sb("up_row", [P, F])
        beta_pad = sb("beta_pad", [P, NB, F])
        w_down = sb("w_down", [P, NB, KC, HID])
        w_up_pad = sb("w_up_pad", [P, NB, F])
        u_pad = sb("u_pad", [P, NB, KC, HID])
        raw = diag[:, :, :, :].rearrange("p a g c -> p (a g c)")
        raw_w = raw[:, 0:1536].rearrange("p (l k f) -> p l k f", l=LAYERS, k=KC)
        w_sq = raw[:, 1536:3072].rearrange("p (l k f) -> p l k f", l=LAYERS, k=KC)
        raw_a = raw[:, 3072:3840].rearrange("p (l k s) -> p l k s", l=LAYERS, k=KC)
        raw_c = raw[:, 3840:3968]
        aff_t = z[:, :, :, :].rearrange("p a g c -> p (a g c)")[:, 0:768].rearrange("p (l f) -> p l f", l=LAYERS)
        gb = x3[:, :, :].rearrange("p k t -> p (k t)")
        gamma_beta = gb[:, 0:640]
        row_sb = z_t[:, :, :, :].rearrange("p a g c -> p (a g c)")[:, 0:640]
        o_w_perm = y[:, :, :].rearrange("p k t -> p (k t)")[:, 0:512].rearrange("p (o c i) -> p o c i", o=KC, c=KC)
        w_dec_sb = gram[:, 1].rearrange("p a h t -> p (a h t)").bitcast(F32)[:, 0:NDEC]
        u_sb = o_rows[:, :, :, :].rearrange("p h x g -> p (h x g)").rearrange("p (k n) -> p k n", n=512)

        psum = ctx.enter_context(nc.psum_tensor("psum", [P, 8, 512], F32))
        SC, OB, PA, PC = 0, 2, 4, 6
        pa = psum[:, PA:PA + 2, :]
        pc = psum[:, PC:PC + 2, :]

        ld_w = sem("ld_w")
        ld_dec = sem("ld_dec")
        ld_bias = sem("ld_bias")
        ld_x = [sem(f"ld_x{p}") for p in range(2)]
        st_rows = sem("st_rows")
        st_u = sem("st_u")
        ld_u = sem("ld_u")
        ld_gate = sem("ld_gate")
        st_keys = [sem(f"st_keys{p}") for p in range(2)]
        ld_keys = [sem(f"ld_keys{p}") for p in range(2)]
        ld_gram = [sem(f"ld_gram{p}") for p in range(2)]
        ld_o = sem("ld_o")
        st_out = sem("st_out")
        ident_0 = sem("ident_0")
        ident_1 = sem("ident_1")
        pads_done = sem("pads_done")
        mask_base = sem("mask_base")
        mask_done = sem("mask_done")
        ld_mask = [sem(f"ld_mask{p}") for p in range(2)]
        diag_zero = sem("diag_zero")
        su_perm = sem("su_perm")
        su_t = sem("su_t")
        su_ev = sem("su_ev")
        su_sq = sem("su_sq")
        su_style = sem("su_style")
        su_rows = sem("su_rows")
        su_rows_ev = sem("su_rows_ev")
        su_st = sem("su_st")
        su_dem = sem("su_dem")
        su_var = sem("su_var")
        su_sqrt = sem("su_sqrt")
        su_tab = sem("su_tab")
        su_u = sem("su_u")
        su_u_ev = sem("su_u_ev")
        su_o0 = sem("su_o0")
        su_uadd = sem("su_uadd")
        cur_a_set = sem("cur_a_set")
        wk_done = sem("wk_done")
        xt_mm = sem("xt_mm")
        xt_ev = sem("xt_ev")
        k_mm = sem("k_mm")
        keys_ev = sem("keys_ev")
        h_done = sem("h_done")
        r1_done = sem("r1_done")
        m_done = sem("m_done")
        l_done = sem("l_done")
        g_mm = sem("g_mm")
        max_done = sem("max_done")
        z_done = sem("z_done")
        exp_done = sem("exp_done")
        sum_done = sem("sum_done")
        inv_done = sem("inv_done")
        norm_done = sem("norm_done")
        zt_done = sem("zt_done")
        diag_done = sem("diag_done")
        av_mm = sem("av_mm")
        o_ev = sem("o_ev")
        cur_c_set = sem("cur_c_set")
        wo_done = sem("wo_done")
        w1_done = sem("w1_done")
        gate_mul_p = sem("gate_mul_p")
        gate_mul = sem("gate_mul")
        u_done = sem("u_done")
        c1_mm = sem("c1_mm")
        c1_ev = sem("c1_ev")
        x1_done = sem("x1_done")
        c2_mm = sem("c2_mm")
        c2_ev = sem("c2_ev")
        clip_done = sem("clip_done")
        x2_done = sem("x2_done")
        c3_mm = sem("c3_mm")
        act_done = sem("act_done")
        c4_mm = sem("c4_mm")
        x3_done = sem("x3_done")
        c5_mm = sem("c5_mm")
        y3_done = sem("y3_done")
        c6_mm = sem("c6_mm")
        x4_done = sem("x4_done")
        c7_mm = sem("c7_mm")
        out_ev = sem("out_ev")

        block = ctx.enter_context(nc.Block())

        def perm(ap):
            return ap.rearrange("p (a c d) -> p c d a", a=H // 2, c=KC)

        def steps(eng, body):
            body(Step(0, 0, 0), "AB")
            body(Step(1, 1, 0), "ABC")
            body(Step(2, 0, 1), "ABC")
            with eng.Fori(0, (STEPS - 4) // 2) as m:
                body(Step(2 * m + 3, 1, m + 1), "ABC")
                body(Step(2 * m + 4, 0, m + 2), "ABC")
            body(Step(STEPS - 1, 1, STEPS // 2 - 1), "BC")
            body(Step(STEPS, 0, STEPS // 2), "C")

        @block.sync
        def _(sp):
            def load(dst, src, s):
                sp.dma_start(dst, src).then_inc(s, 16)

            with nc.allow_non_contiguous_dma(reason="bias columns"):
                load(raw_c[0:B, :], cond, ld_w)
                for n, w in enumerate((ka_w, oa_w, la_w)):
                    load(raw_a[:, n], w.rearrange("(k p) s -> p k s", p=P), ld_w)
                for c in range(KC):
                    load(raw_w[:, 0, c], k_w.rearrange("(a c d) i -> c d a i", a=H // 2, c=KC)[c], ld_w)
                for n, w in ((1, o_w), (2, w1)):
                    load(raw_w[:, n], w.rearrange("(k p) i -> p k i", p=P), ld_w)
                load(x_in[:, 0], x_rows[0:T, :].rearrange("(q p) f -> p q f", p=P), ld_x[0])
                for n, (v, permuted) in enumerate(((ka_b, False), (oa_b, True), (la_b, False),
                                                   (k_b, True), (o_b, False), (b1, False))):
                    for c in range(KC):
                        if permuted:
                            src = v.rearrange("(a c d) -> c d a", a=H // 2, c=KC)[c]
                        else:
                            src = v.rearrange("(c p) -> c p", c=KC)[c]
                        load(biases[:, n, c:c + 1], src, ld_bias)
                load(down_sb[:, :, :], down.rearrange("(k p) h -> p k h", p=P), ld_w)
                for n, (w, o) in enumerate(((dgamma, 0), (dbeta, HID), (ugamma, 2 * HID), (ubeta, 2 * HID + F))):
                    load(gamma_beta[:, o:o + w.shape[1]], w, ld_w)
                load(w_dec_sb, w_dec, ld_dec)
                for c in range(KC):
                    load(b_dec_t[:, c, :], b_dec[c * P * RANK:(c + 1) * P * RANK].rearrange("(p k) -> p k", k=RANK), ld_dec)
                sp.wait_ge(pads_done, 7)
                for b in range(NB):
                    load(up_pad[HID * b:HID * (b + 1), b, :], up, ld_dec)
                    load(v_pad[64 * b:64 * b + RANK, b, :], v_mat, ld_dec)
                    load(b_dec_c[64 * b:64 * b + RANK, :], b_dec[F * RANK:(F + 1) * RANK].rearrange("(k o) -> k o", o=1), ld_dec)
                sp.wait_ge(su_rows_ev, 2)
                sp.dma_start(rows_dram, row_sb[0:B, :]).then_inc(st_rows, 16)

            def decoder_out():
                sp.wait_ge(su_u_ev, 3)
                for c in range(4):
                    dst = u_dram.rearrange("b (k c n) -> c b k n", c=4, n=512)[c]
                    if c < 3:
                        sp.dma_start(dst, u_sb[32 * c:32 * c + B, :, :]).then_inc(st_u, 16)
                    else:
                        sp.dma_start(dst[:, 0:3, :], u_sb[96:96 + B, 0:3, :]).then_inc(st_u, 16)
                        last = NDEC - (UCH - 1) * 512
                        sp.dma_start(dst[:, 3, 0:last], u_sb[96:96 + B, 3, 0:last]).then_inc(st_u, 16)
                sp.wait_ge(st_u, 16 * 5)
                with nc.allow_non_contiguous_dma(reason="bias columns"):
                    for c in range(KC):
                        src = u_dram[:, c * P * RANK:(c + 1) * P * RANK].rearrange("b (p k) -> p b k", k=RANK)
                        sp.dma_start(u_all[:, :, c, :], src).then_inc(ld_u, 16)
                    for b in range(NB):
                        src = u_dram.rearrange("(s b) n -> b n s", b=NB)[b][F * RANK:(F + 1) * RANK, :]
                        sp.dma_start(ybias[64 * b:64 * b + RANK, :], src).then_inc(ld_u, 16)

            def gates(s):
                used, *first = held(sp, 2 * s.i, *(NB * s.i + b for b in range(NB)))
                rows = [rows_dram[bass.ds(first[b], 1), :] for b in range(NB)]
                wait(sp, gate_mul, used)
                for b, row in enumerate(rows):
                    half = slice(HID * b, HID * (b + 1))
                    sp.dma_start(up_row[half, :], row[:, 2 * HID:2 * HID + F].to_broadcast([HID, F]))\
                        .then_inc(ld_gate, 16)
                    sp.dma_start(beta_pad[half, b, :], row[:, 2 * HID + F:2 * HID + 2 * F].to_broadcast([HID, F]))\
                        .then_inc(ld_gate, 16)
                    sp.dma_start(down_row[:, b, :, :].rearrange("p a h -> p (a h)"),
                                 row[:, 0:2 * HID].to_broadcast([P, 2 * HID])).then_inc(ld_gate, 16)

            def mask_rows(par):
                for side in range(2):
                    sp.dma_start(gram[96:98, par, side],
                                 mask[96:98, side, :].unsqueeze(1).to_broadcast([2, H, T]))\
                        .then_inc(ld_mask[par], 16)

            def spread(a):
                evacuated, read, split, stored = held(sp, 4 * (a.i + 1), CH * (a.i - 1), a.i + 1, 16 * (a.uses + 1))
                sp.wait_ge(keys_ev, evacuated)
                sp.dma_start(keys_dram[a.par].rearrange("d (a b) n -> (d a) (b n)", b=KC),
                             keys[:, :, :].rearrange("p b n -> p (b n)")).then_inc(st_keys[a.par], 16)
                wait(sp, g_mm, read)
                if isinstance(a.i, int) and a.i == 1:
                    sp.wait_ge(su_u, UCH)
                    mask_rows(1)
                for c, done in (("h", h_done), ("m", m_done), ("l", l_done)):
                    sp.wait_ge(done, split)
                    for side, order in enumerate((LEFT_PARTS, RIGHT_PARTS)):
                        for g, o in enumerate(order):
                            if o == c:
                                sp.dma_start(gram[16 * g:16 * g + 16, a.par, side, :, :], part[c][:, :, :])\
                                    .then_inc(ld_gram[a.par], 16)
                    if c == "h":
                        sp.wait_ge(st_keys[a.par], stored)
                        wait(sp, av_mm, read)
                        for xt in range(XT):
                            src = keys_dram[a.par].rearrange("d j n -> j d n")[:, :, xt * G:(xt + 1) * G]
                            first = 32 * (xt % 4) + xt // 4
                            sp.dma_start(keys_v[first:first + 2 * H - 1:2, a.par, :, :], src)\
                                .then_inc(ld_keys[a.par], 16)

            def body(s, stages):
                if "A" in stages:
                    a = following(s)
                    first, used = held(sp, a.i * T, 2 * (a.i - 1))
                    rows = x_rows[bass.ds(first, T), :].rearrange("(q p) f -> p q f", p=P)
                    wait(sp, xt_mm, used)
                    sp.dma_start(x_in[:, a.par], rows)\
                        .then_inc(ld_x[a.par], 16)
                if "C" in stages:
                    c = preceding(s)
                    sp.wait_ge(o_ev, CH * (c.i + 1))
                    for t in range(CH):
                        sp.dma_start(o_t[:, :, t].rearrange("p k x g -> p k (x g)"),
                                     o_rows[32 * t:32 * t + D].rearrange("p h x g -> p h (x g)")).then_inc(ld_o, 16)
                if "A" in stages:
                    spread(following(s))
                if isinstance(s.i, int) and s.i == 0:
                    decoder_out()
                if "B" in stages:
                    if isinstance(s.i, int) and s.i == 0:
                        sp.wait_ge(st_rows, 16)
                    gates(s)
                if "C" in stages:
                    c = preceding(s)
                    first, ready = held(sp, c.i * T, 2 * (c.i + 1))
                    rows = out_rows[bass.ds(first, T), :].rearrange("(q p) f -> p q f", p=P)
                    sp.wait_ge(out_ev, ready)
                    sp.dma_start(rows, out_sb[:, :, :]).then_inc(st_out, 16)

            sp.wait_ge(mask_done, 2)
            mask_rows(0)
            spread(Step(0, 0, 0))
            steps(sp, body)
            sp.wait_ge(st_out, 16 * STEPS)

        @block.gpsimd
        def _(pool):
            pool.memset(ident[:, :], 0.0).then_inc(ident_0, 1)
            pool.wait_ge(ident_0, 1)
            pool.affine_select(out=ident[:, :], in_=ident[:, :], compare_op=ALU.not_equal, fill=1.0,
                               base=0, pattern=[[-1, P]], channel_multiplier=1).then_inc(ident_1, 1)
            pool.memset(cond_t[:, :], 0.0).then_inc(pads_done, 1)
            pool.memset(v_pad[:, :, :], 0.0).then_inc(pads_done, 1)
            pool.memset(b_dec_c[:, :], 0.0).then_inc(pads_done, 1)
            pool.memset(ybias[:, :], 0.0).then_inc(pads_done, 1)
            pool.memset(u_pad[:, :, :, :], 0.0).then_inc(pads_done, 1)
            pool.memset(beta_pad[:, :, :], 0.0).then_inc(pads_done, 1)
            pool.memset(up_pad[:, :, :], 0.0).then_inc(pads_done, 1)

            left, right = (mask[96:98, side, :].rearrange("p (t g) -> p t g", t=2) for side in range(2))
            pool.wait_ge(pads_done, 7)
            pool.memset(left, 1.0).then_inc(mask_base, 1)
            pool.memset(right, 0.0).then_inc(mask_base, 1)
            pool.wait_ge(mask_base, 2)
            for ap, fill in ((left, 0.0), (right, NEG)):
                pool.affine_select(out=ap, in_=ap, compare_op=ALU.is_equal, fill=fill, base=0,
                                   pattern=[[-1, 2], [0, N]], channel_multiplier=1).then_inc(mask_done, 1)
            pool.wait_ge(mask_done, 2)
            pool.wait_ge(su_dem, 1)
            pool.memset(diag[:, :, :, :], 0.0).then_inc(diag_zero, 1)

            def residue(a):
                pool.wait_ge(h_done, a.i + 1)
                wait(pool, l_done, a.i)
                pool.tensor_tensor(rest[:, :, :], keys[:, :, :], part["h"][:, :, :], ALU.subtract)\
                    .then_inc(r1_done, 1)

            def normalise(s, n):
                pool.wait_ge(inv_done, CH * s.i + n + 1)
                pool.wait_ge(exp_done, CH * s.i + n + 1)
                b = n % 2
                pool.tensor_tensor(z[:, b], z[:, b], row_inv[:, b, :].unsqueeze(2).to_broadcast([P, GC, 32]),
                                   ALU.mult).then_inc(norm_done, 1)

            def body(s, stages):
                c = preceding(s)
                if "C" in stages:
                    pool.wait_ge(ld_gate, 96 * (c.i + 1))
                    wait(pool, c4_mm, 2 * c.i)
                    for b in range(NB):
                        gam = down_row[:, b, 0, :].unsqueeze(1).to_broadcast([P, KC, HID])
                        pool.tensor_tensor(w_down[:, b], down_sb[:, :, :], gam, ALU.mult).then_inc(gate_mul_p, 1)
                    pool.tensor_tensor(w_up_pad[:, :, :], up_pad[:, :, :],
                                       up_row[:, :].unsqueeze(1).to_broadcast([P, NB, F]), ALU.mult)\
                        .then_inc(gate_mul_p, 1)
                    pool.wait_ge(gate_mul_p, 3 * (c.i + 1))
                    for b in range(NB):
                        beta = down_row[:, b, 1, :].unsqueeze(1).to_broadcast([P, KC, HID])
                        mul = pool.tensor_tensor(w_down[:, b], w_down[:, b], beta, ALU.add)
                    mul.then_inc(gate_mul, 1)
                    pool.tensor_tensor(w_up_pad[:, :, :], w_up_pad[:, :, :], beta_pad[:, :, :], ALU.add)\
                        .then_inc(gate_mul, 1)
                if "B" in stages:
                    normalise(s, 0)
                if "C" in stages:
                    pool.wait_ge(c1_ev, 4 * (c.i + 1))
                    wait(pool, x2_done, c.i)
                    pool.tensor_tensor(x1[:, :, :], y[:, :, :], x_t[:, c.par], ALU.add).then_inc(x1_done, 1)
                if "B" in stages:
                    normalise(s, 1)
                if "A" in stages:
                    residue(following(s))
                if "B" in stages:
                    normalise(s, 2)
                if "C" in stages:
                    pool.wait_ge(clip_done, c.i + 1)
                    wait(pool, x3_done, 2 * c.i)
                    pool.tensor_tensor(x2[:, :, :], y[:, :, :], x1[:, :, :], ALU.add).then_inc(x2_done, 1)
                if "B" in stages:
                    normalise(s, 3)
                if isinstance(s.i, int) and s.i == 0:
                    pool.wait_ge(ld_u, 64)
                    pool.wait_ge(ld_dec, 16 * 9)
                    pool.tensor_tensor(u_all[:, :, :, :], u_all[:, :, :, :],
                                       b_dec_t[:, :, :].rearrange("p c k -> p (c k)").unsqueeze(1)
                                       .to_broadcast([P, B, KC * RANK]).rearrange("p b (c k) -> p b c k", c=KC),
                                       ALU.add).then_inc(su_uadd, 1)
                    pool.tensor_tensor(table_c[:, :, 16], ybias[:, :], b_dec_c[:, :].to_broadcast([P, STEPS]),
                                       ALU.add).then_inc(su_uadd, 1)

            residue(Step(0, 0, 0))
            steps(pool, body)

        @block.scalar
        def _(act):
            for n in range(LAYERS):
                act.wait_ge(su_t, 3 + n)
                act.activation(w_t[:, n].rearrange("p k f -> p (k f)"), psum[:, 2 + n, :], ACT.Copy)\
                    .then_inc(su_ev, 1)
                act.activation(w_sq[:, n].rearrange("p k f -> p (k f)"), psum[:, 2 + n, :], ACT.Square)\
                    .then_inc(su_sq, 1)
            act.wait_ge(su_rows, 1)
            act.activation(row_sb[0:32, 0:2 * HID], psum[0:32, 7, 0:2 * HID], ACT.Copy).then_inc(su_rows_ev, 1)
            act.activation(row_sb[0:32, 2 * HID:640], psum[0:32, 6, :], ACT.Copy).then_inc(su_rows_ev, 1)
            act.wait_ge(su_var, 1)
            act.activation(eps_t[:, :], eps_t[:, :], ACT.Sqrt).then_inc(su_sqrt, 1)

            def x_evacuate(a):
                act.wait_ge(xt_mm, 2 * (a.i + 1))
                wait(act, x1_done, a.i - 1)
                act.activation(x_t[:, a.par], pa, ACT.Copy).then_inc(xt_ev, 1)

            def keys_evacuate(a):
                if isinstance(a.i, int) and a.i == 0:
                    act.wait_ge(ld_bias, 16 * 12)
                else:
                    before = preceding(a)
                    act.wait_ge(st_keys[before.par], 16 * (before.uses + 1))
                    act.wait_ge(r1_done, a.i)
                act.wait_ge(cur_a_set, a.i + 1)
                for c in range(KC):
                    act.wait_ge(k_mm, 2 * a.i + c + 1)
                    for b in range(NB):
                        t = slice(N * b, N * (b + 1))
                        act.activation(keys[:, c, t], pa[:, c, t], ACT.Identity, bias=biases[:, 3, c:c + 1],
                                       scale=cur_a[:, 4 + 2 * c + b:5 + 2 * c + b]).then_inc(keys_ev, 1)

            def exponent(s, n):
                act.wait_ge(z_done, CH * s.i + n + 1)
                b = n % 2
                act.activation(z[:, b], z[:, b], ACT.Exp, scale=D ** -0.5).then_inc(exp_done, 1)

            def spread_diagonal(s, n):
                act.wait_ge(zt_done, CH * s.i + n + 1)
                wait(act, av_mm, CH * s.i + n - 1)
                if isinstance(s.i, int) and s.i == 0 and n == 0:
                    act.wait_ge(diag_zero, 1)
                b = n % 2
                for q in range(4):
                    r = slice(32 * q, 32 * q + 32)
                    act.activation(diag[r, b, :, r], z_t[r, b], ACT.Copy).then_inc(diag_done, 1)

            def linear_evacuate(c, mm, ev, bias, col):
                for o in range(KC):
                    act.wait_ge(mm, 2 * c.i + o + 1)
                    for b in range(NB):
                        t = slice(N * b, N * (b + 1))
                        act.activation(y[:, o, t], pc[:, o, t], ACT.Identity, bias=biases[:, bias, o:o + 1],
                                       scale=cur_c[:, col + 2 * o + b:col + 1 + 2 * o + b]).then_inc(ev, 1)

            def body(s, stages):
                c = preceding(s)
                if "C" in stages:
                    act.wait_ge(cur_c_set, c.i + 1)
                    wait(act, x2_done, c.i)
                    linear_evacuate(c, c1_mm, c1_ev, 4, 4)
                if "B" in stages:
                    exponent(s, 0)
                if "A" in stages:
                    x_evacuate(following(s))
                if "B" in stages:
                    exponent(s, 1)
                    spread_diagonal(s, 0)
                if "A" in stages:
                    keys_evacuate(following(s))
                if "C" in stages:
                    act.wait_ge(x1_done, c.i + 1)
                    linear_evacuate(c, c2_mm, c2_ev, 5, 12)
                if "B" in stages:
                    exponent(s, 2)
                    spread_diagonal(s, 1)
                    exponent(s, 3)
                if "C" in stages:
                    act.wait_ge(c3_mm, c.i + 1)
                    wait(act, c4_mm, 2 * c.i)
                    act.activation(act2[:, :], pc[:, 0, 0:N], ACT.Relu).then_inc(act_done, 1)
                if "B" in stages:
                    spread_diagonal(s, 2)
                if "C" in stages:
                    act.wait_ge(c5_mm, c.i + 1)
                    wait(act, c6_mm, 2 * c.i)
                    act.activation(y3[:, :], pc[:, 0, 0:N], ACT.Identity, bias=cur_c[:, 16:17]).then_inc(y3_done, 1)
                if "B" in stages:
                    spread_diagonal(s, 3)
                if "C" in stages:
                    wait(act, st_out, 16 * c.i)
                    for o in range(2):
                        act.wait_ge(c7_mm, 2 * c.i + o + 1)
                        act.activation(out_sb[:, 2 * o:2 * o + 2, :].rearrange("p q f -> p (q f)"), pc[:, o, :],
                                       ACT.Copy).then_inc(out_ev, 1)

            x_evacuate(Step(0, 0, 0))
            keys_evacuate(Step(0, 0, 0))
            steps(act, body)

        @block.vector
        def _(dve):
            dve.wait_ge(ld_w, 16 * 13)
            for o in range(KC):
                dve.tensor_copy(o_w_perm[:, o].rearrange("p c (d a) -> p c d a", d=D), perm(raw_w[:, 1, o, :]))\
                    .then_inc(su_perm, 1)
            dve.wait_ge(su_t, 2)
            dve.wait_ge(pads_done, 7)
            flat = psum[:, 0:2, :].rearrange("p k n -> p (k n)")
            dve.tensor_copy(aff_t[:, 0, :], flat[:, 0:F]).then_inc(su_ev, 1)
            dve.tensor_copy(aff_t[:, 1, :].rearrange("p (c d a) -> p c d a", c=KC, d=D), perm(flat[:, F:2 * F]))\
                .then_inc(su_ev, 1)
            dve.tensor_scalar(aff_t[:, 2, :], flat[:, 2 * F:3 * F], GAIN, None, ALU.mult).then_inc(su_ev, 1)
            dve.tensor_copy(cond_t[:, 0:B], flat[:, 3 * F:3 * F + B]).then_inc(su_ev, 1)
            dve.wait_ge(su_style, 1)
            dve.wait_ge(ld_bias, 16 * 12)
            dve.tensor_tensor(style[:, :, :], psum[:, 5, 0:96].rearrange("p (k b) -> p k b", b=B),
                              biases[:, 0:3, :].rearrange("p l c -> p (l c)").unsqueeze(2).to_broadcast([P, 6, B]),
                              ALU.add).then_inc(su_st, 1)
            dve.wait_ge(su_st, 1)
            dve.tensor_tensor(style2[:, :, :], style[:, :, :], style[:, :, :], ALU.mult).then_inc(su_st, 1)

            def by_step(ap):
                return ap.rearrange("p c (s b) -> p c s b", b=NB)

            def columns(table, at):
                return table[:, :, at:at + 4].rearrange("p s (c b) -> p c s b", b=NB)

            dve.tensor_copy(columns(table_a, 0), by_step(style[:, 0:2, :])).then_inc(su_tab, 1)
            dve.tensor_copy(columns(table_c, 0), by_step(style[:, 2:4, :])).then_inc(su_tab, 1)
            dve.tensor_copy(columns(table_c, 8), by_step(style[:, 4:6, :])).then_inc(su_tab, 1)
            dve.wait_ge(su_dem, 1)
            dve.tensor_scalar(eps_t[:, :], psum[:, 0, 0:96], EPS, None, ALU.add).then_inc(su_var, 1)
            dve.wait_ge(su_sqrt, 1)
            dem = style2[:, :, :].rearrange("p k b -> p (k b)")
            dve.reciprocal(dem, eps_t[:, :]).then_inc(su_st, 1)
            dve.wait_ge(su_st, 3)
            dve.tensor_copy(columns(table_a, 4), by_step(style2[:, 0:2, :])).then_inc(su_tab, 1)
            dve.tensor_copy(columns(table_c, 4), by_step(style2[:, 2:4, :])).then_inc(su_tab, 1)
            dve.tensor_copy(columns(table_c, 12), by_step(style2[:, 4:6, :])).then_inc(su_tab, 1)

            def modulate(n, cur, col, done):
                for b in range(NB):
                    for c in range(KC):
                        dve.tensor_scalar(w_mod[n][:, b, c, :], w_t[:, n, c, :],
                                          cur[:, col + 2 * c + b:col + 1 + 2 * c + b], None, ALU.mult)\
                            .then_inc(done, 1)

            def prepare_a(a):
                wait(dve, keys_ev, 4 * a.i)
                dve.tensor_copy(cur_a[:, :], table_a[:, a.i, :]).then_inc(cur_a_set, 1)
                dve.wait_ge(cur_a_set, a.i + 1)
                wait(dve, k_mm, 2 * a.i)
                modulate(0, cur_a, 0, wk_done)

            def high(a):
                dve.wait_ge(keys_ev, 4 * (a.i + 1))
                if not (isinstance(a.i, int) and a.i == 0):
                    before = preceding(a)
                    dve.wait_ge(ld_gram[before.par], 16 * 12 * (before.uses + 1))
                dve.tensor_copy(part["h"][:, :, :], keys[:, :, :]).then_inc(h_done, 1)

            def middle_low(a):
                dve.wait_ge(r1_done, a.i + 1)
                dve.tensor_copy(part["m"][:, :, :], rest[:, :, :]).then_inc(m_done, 1)
                dve.wait_ge(m_done, a.i + 1)
                dve.tensor_tensor(part["l"][:, :, :], rest[:, :, :], part["m"][:, :, :], ALU.subtract)\
                    .then_inc(l_done, 1)

            def shift(s, n):
                k = CH * s.i + n
                b = n % 2
                dve.wait_ge(g_mm, k + 1)
                scores = psum[:, SC + b, :].rearrange("p (g j) -> p g j", j=32)
                dve.tensor_reduce(row_max[:, :], scores, AX_X, ALU.max).then_inc(max_done, 1)
                dve.wait_ge(max_done, k + 1)
                wait(dve, zt_done, k - 1)
                dve.tensor_tensor(z[:, b], scores, row_max[:, :].unsqueeze(2).to_broadcast([P, GC, 32]),
                                  ALU.subtract).then_inc(z_done, 1)

            def row_sums(s, n):
                k = CH * s.i + n
                b = n % 2
                dve.wait_ge(exp_done, k + 1)
                dve.tensor_reduce(row_sum[:, :], z[:, b], AX_X, ALU.add).then_inc(sum_done, 1)
                dve.wait_ge(sum_done, k + 1)
                wait(dve, norm_done, k - 1)
                dve.reciprocal(row_inv[:, b, :], row_sum[:, :]).then_inc(inv_done, 1)

            def transpose(s, n):
                k = CH * s.i + n
                b = n % 2
                dve.wait_ge(norm_done, k + 1)
                wait(dve, diag_done, 4 * (k - 1))
                dve.transpose(z_t[:, b].rearrange("p g j -> p (g j)"), z[:, b].rearrange("p g j -> p (g j)"))\
                    .then_inc(zt_done, 1)

            def o_evacuate(s, n):
                k = CH * s.i + n
                dve.wait_ge(av_mm, k + 1)
                if n == 0:
                    wait(dve, ld_o, 64 * s.i)
                    if isinstance(s.i, int) and s.i == 0:
                        dve.wait_ge(st_u, 16 * 5)
                src = psum[:, OB + n % 2, :].rearrange("p (r q h) -> p r q h", r=4, q=4)
                dst = o_rows[:, :, :, n * 4:n * 4 + 4].rearrange("p h (t q) r -> p r q (h t)", t=2)
                dve.tensor_copy(dst, src).then_inc(o_ev, 1)

            def prepare_c(c):
                wait(dve, c2_ev, 4 * c.i)
                wait(dve, y3_done, c.i)
                dve.tensor_copy(cur_c[:, :], table_c[:, c.i, :]).then_inc(cur_c_set, 1)
                dve.wait_ge(cur_c_set, c.i + 1)
                wait(dve, c2_mm, 2 * c.i)
                modulate(1, cur_c, 0, wo_done)
                modulate(2, cur_c, 8, w1_done)
                wait(dve, c5_mm, c.i)
                dve.tensor_copy(u_pad[:, :, :, 0:RANK], u_all[:, bass.ds(NB * c.i, NB), :, :]).then_inc(u_done, 1)

            def body(s, stages):
                c = preceding(s)
                if isinstance(s.i, int) and s.i == 0:
                    dve.wait_ge(su_u, UCH)
                    dve.tensor_copy(u_sb[:, 0:3, :], psum[:, 0:3, :]).then_inc(su_u_ev, 1)
                    dve.tensor_copy(u_sb[0:96, 3, :], psum[0:96, 3, :]).then_inc(su_u_ev, 1)
                    last = NDEC - (UCH - 1) * 512
                    dve.tensor_copy(u_sb[96:128, 3, 0:last], psum[96:128, 3, 0:last]).then_inc(su_u_ev, 1)
                    dve.wait_ge(su_u_ev, 3)
                    dve.memset(psum[:, OB:OB + 2, :], 0.0).then_inc(su_o0, 1)
                if "C" in stages:
                    prepare_c(c)
                if "A" in stages:
                    prepare_a(following(s))
                if "B" in stages:
                    shift(s, 0)
                    row_sums(s, 0)
                    shift(s, 1)
                    transpose(s, 0)
                    row_sums(s, 1)
                if "A" in stages:
                    high(following(s))
                    middle_low(following(s))
                if "B" in stages:
                    transpose(s, 1)
                    o_evacuate(s, 0)
                if "C" in stages:
                    dve.wait_ge(c2_ev, 4 * (c.i + 1))
                    dve.tensor_scalar(y[:, :, :], y[:, :, :], -CLAMP, CLAMP, ALU.max, ALU.min)\
                        .then_inc(clip_done, 1)
                if "B" in stages:
                    shift(s, 2)
                    o_evacuate(s, 1)
                    row_sums(s, 2)
                    transpose(s, 2)
                    shift(s, 3)
                    row_sums(s, 3)
                    o_evacuate(s, 2)
                if "C" in stages:
                    wait(dve, c7_mm, 2 * c.i)
                    for o in range(KC):
                        dve.wait_ge(c4_mm, 2 * c.i + o + 1)
                        dve.scalar_tensor_tensor(x3[:, o, :], x2[:, o, :], 2.0, pc[:, o, :], ALU.mult, ALU.add)\
                            .then_inc(x3_done, 1)
                if "B" in stages:
                    transpose(s, 3)
                if "C" in stages:
                    for o in range(KC):
                        dve.wait_ge(c6_mm, 2 * c.i + o + 1)
                        dve.tensor_tensor(x3[:, o, :], pc[:, o, :], x3[:, o, :], ALU.add).then_inc(x4_done, 1)
                if "B" in stages:
                    o_evacuate(s, 3)
                if isinstance(s.i, int) and s.i == 0:
                    dve.wait_ge(su_uadd, 2)

            dve.wait_ge(su_tab, 6)
            prepare_a(Step(0, 0, 0))
            high(Step(0, 0, 0))
            middle_low(Step(0, 0, 0))
            steps(dve, body)

        @block.tensor
        def _(pe):
            mm = nc.tensor.matmul
            pe.wait_ge(ident_1, 1)
            pe.wait_ge(ld_w, 16 * 13)
            slot = psum[:, 0:5, :].rearrange("p k (s n) -> p (k s) n", n=P)
            for n in range(LAYERS):
                for c in range(KC):
                    last = nc.tensor.transpose(slot[:, 2 * n + c, :], raw_a[:, n, c, :], ident[:, :])
                    if 2 * n + c == 3:
                        last.then_inc(su_t, 1)
            nc.tensor.transpose(slot[:, 6, 0:B], raw_c[0:B, :], ident[0:B, 0:B]).then_inc(su_t, 1)
            pe.wait_ge(su_perm, 2)
            for n in range(LAYERS):
                for c in range(KC):
                    for o in range(KC):
                        src = raw_w[:, n, o, :]
                        src = o_w_perm[:, o, c, :] if n == 1 else src[:, c * P:(c + 1) * P]
                        last = nc.tensor.transpose(slot[:, 8 + 4 * n + 2 * c + o, :], src, ident[:, :])
                last.then_inc(su_t, 1)
            pe.wait_ge(su_ev, 7)
            for n in range(LAYERS):
                for c in range(KC):
                    src = aff_t[:, n, c * P:(c + 1) * P]
                    k = (2 * n + c) * B
                    last = mm(psum[:, 5, k:k + B], src, cond_t[:, 0:B], start=True, stop=True)
            last.then_inc(su_style, 1)
            mm(psum[0:32, 7, 0:2 * HID], cond_t[:, :], gamma_beta[:, 0:2 * HID], start=True, stop=True)
            mm(psum[0:32, 6, :], cond_t[:, :], gamma_beta[:, 2 * HID:640], start=True, stop=True).then_inc(su_rows, 1)
            pe.wait_ge(su_st, 2)
            pe.wait_ge(su_sq, LAYERS)
            for n in range(LAYERS):
                for o in range(KC):
                    k = (2 * n + o) * B
                    for c in range(KC):
                        last = mm(psum[:, 0, k:k + B], w_sq[:, n, c, o * P:(o + 1) * P], style2[:, 2 * n + c, :],
                                  start=(c == 0), stop=(c == KC - 1))
            last.then_inc(su_dem, 1)

            def x_transposes(a):
                pe.wait_ge(ld_x[a.par], 16 * (a.uses + 1))
                wait(pe, keys_ev, 4 * a.i)
                for c in range(KC):
                    for q in range(Q):
                        last = nc.tensor.transpose(pa[:, c, q * P:(q + 1) * P],
                                                   x_in[:, a.par, q, c * P:(c + 1) * P], ident[:, :])
                    last.then_inc(xt_mm, 1)

            def project_keys(a):
                pe.wait_ge(xt_ev, a.i + 1)
                pe.wait_ge(wk_done, 4 * (a.i + 1))
                for o in range(KC):
                    for b in range(NB):
                        for c in range(KC):
                            last = mm(pa[:, o, N * b:N * (b + 1)], w_mod[0][:, b, c, o * P:(o + 1) * P],
                                      x_t[:, a.par, c, N * b:N * (b + 1)], start=(c == 0), stop=(c == KC - 1))
                    last.then_inc(k_mm, 1)

            def decoder():
                pe.wait_ge(ld_dec, 16 * 9)
                pe.wait_ge(su_var, 1)
                for k in range(UCH):
                    q = k % 4
                    w = min(512, NDEC - 512 * k)
                    mm(psum[32 * q:32 * q + 32, k // 4, 0:w], cond_t[:, :], w_dec_sb[:, 512 * k:512 * k + w],
                       start=True, stop=True).then_inc(su_u, 1)

            def scores(s, n):
                if n == 0:
                    pe.wait_ge(ld_gram[s.par], 16 * 12 * (s.uses + 1))
                if isinstance(s.i, int) and s.i == 0 and n == 0:
                    pe.wait_ge(ld_mask[0], 32)
                    pe.wait_ge(su_u_ev, 3)
                wait(pe, z_done, CH * s.i + n - 1)
                left, right = (gram[0:98, s.par, side].rearrange("p h (t m) -> p (h t) m", t=2) for side in range(2))
                for g in range(GC):
                    grp = (g // 4) * GC + n * 4 + g % 4
                    for q in range(4):
                        last = mm(psum[32 * q:32 * q + 32, SC + n % 2, 32 * g:32 * g + 32],
                                  left[:, :, q * G + grp], right[:, :, q * G + grp],
                                  start=True, stop=True)
                last.then_inc(g_mm, 1)

            def values(s, n):
                if n == 0:
                    pe.wait_ge(ld_keys[s.par], 16 * XT * (s.uses + 1))
                    if isinstance(s.i, int) and s.i == 0:
                        pe.wait_ge(su_o0, 1)
                k = CH * s.i + n
                pe.wait_ge(diag_done, 4 * (k + 1))
                wait(pe, o_ev, k - 1)
                for r in range(4):
                    for c in range(4):
                        last = mm(psum[32 * c:32 * c + D, OB + n % 2, P * r:P * (r + 1)],
                                  keys_v[:, s.par, :, c * GC + n * 4 + r], diag[:, n % 2, c * 4 + r, :],
                                  start=True, stop=True)
                last.then_inc(av_mm, 1)

            def project_o(c):
                pe.wait_ge(ld_o, 64 * (c.i + 1))
                pe.wait_ge(wo_done, 4 * (c.i + 1))
                wait(pe, out_ev, 2 * c.i)
                for o in range(KC):
                    for b in range(NB):
                        for k in range(KC):
                            src = o_t[:, k, :, 4 * b:4 * b + 4, :].rearrange("p c x g -> p x c g")
                            last = mm(pc[:, o, N * b:N * (b + 1)], w_mod[1][:, b, k, o * P:(o + 1) * P], src,
                                      start=(k == 0), stop=(k == KC - 1))
                    last.then_inc(c1_mm, 1)

            def layer1(c):
                pe.wait_ge(x1_done, c.i + 1)
                pe.wait_ge(w1_done, 4 * (c.i + 1))
                pe.wait_ge(c1_ev, 4 * (c.i + 1))
                for o in range(KC):
                    for b in range(NB):
                        for k in range(KC):
                            last = mm(pc[:, o, N * b:N * (b + 1)], w_mod[2][:, b, k, o * P:(o + 1) * P],
                                      x1[:, k, N * b:N * (b + 1)], start=(k == 0), stop=(k == KC - 1))
                    last.then_inc(c2_mm, 1)

            def low_rank_in(w, src, done):
                for k in range(KC):
                    for b in range(NB):
                        last = mm(pc[64 * b:64 * b + 64, 0, 0:N], w[:, b, k, :], src[:, k, N * b:N * (b + 1)],
                                  start=(k == 0), stop=(k == KC - 1))
                last.then_inc(done, 1)

            def low_rank_out(w, src, done):
                for o in range(KC):
                    for b in range(NB):
                        last = mm(pc[:, o, N * b:N * (b + 1)], w[:, b, o * P:(o + 1) * P], src[:, :],
                                  start=True, stop=True)
                    last.then_inc(done, 1)

            def body(s, stages):
                c = preceding(s)
                b = "B" in stages
                if b:
                    scores(s, 0)
                if "C" in stages:
                    project_o(c)
                if b:
                    scores(s, 1)
                if "A" in stages:
                    x_transposes(following(s))
                    project_keys(following(s))
                if b:
                    values(s, 0)
                if "C" in stages:
                    layer1(c)
                if b:
                    scores(s, 2)
                    values(s, 1)
                    scores(s, 3)
                if "C" in stages:
                    pe.wait_ge(x2_done, c.i + 1)
                    pe.wait_ge(gate_mul, 2 * (c.i + 1))
                    low_rank_in(w_down, x2, c3_mm)
                if b:
                    values(s, 2)
                if "C" in stages:
                    pe.wait_ge(act_done, c.i + 1)
                    low_rank_out(w_up_pad, act2, c4_mm)
                    pe.wait_ge(x3_done, 2 * (c.i + 1))
                    pe.wait_ge(u_done, c.i + 1)
                    low_rank_in(u_pad, x3, c5_mm)
                    pe.wait_ge(y3_done, c.i + 1)
                    low_rank_out(v_pad, y3, c6_mm)
                if b:
                    values(s, 3)
                if isinstance(s.i, int) and s.i == 0:
                    pe.wait_ge(ld_mask[1], 32)
                if "C" in stages:
                    for o in range(2):
                        if o == 0:
                            pe.wait_ge(x4_done, 2 * (c.i + 1))
                        for q in range(2 * o, 2 * o + 2):
                            for k in range(KC):
                                last = nc.tensor.transpose(pc[:, o, (q % 2) * F + k * P:(q % 2) * F + (k + 1) * P],
                                                           x3[:, k, q * P:(q + 1) * P], ident[:, :])
                        last.then_inc(c7_mm, 1)

            x_transposes(Step(0, 0, 0))
            project_keys(Step(0, 0, 0))
            decoder()
            steps(pe, body)


_INS = ['x', 'cond_512', 'L0_cond_k_aff_w', 'L0_cond_k_aff_b', 'L0_cond_k_w', 'L0_cond_k_b', 'L0_cond_o_aff_w',
        'L0_cond_o_aff_b', 'L0_cond_o_w', 'L0_cond_o_b', 'L1_cond_weight', 'L1_cond_bias', 'L1_cond_affine_w',
        'L1_cond_affine_b', 'L2_cond_down_project', 'L2_cond_down_gamma', 'L2_cond_down_beta',
        'L2_cond_up_project', 'L2_cond_up_gamma', 'L2_cond_up_beta', 'L3_cond_W_dec', 'L3_cond_b_dec', 'L3_cond_V']
_OUTS = [((16, 256, 256), 'float32')]


def kernel(**inputs):
    import numpy as _np
    import concourse.bacc as _bacc
    from concourse import mybir as _mybir
    from concourse.bass_utils import run_bass_kernel_spmd as _run

    nc = _bacc.Bacc("TRN2", target_bir_lowering=False, num_devices=1)
    arrays, args = {}, []
    for name in _INS:
        a = _np.ascontiguousarray(inputs[name])
        arrays[f"in_{name}_dram"] = a
        args.append(nc.dram_tensor(f"in_{name}_dram", a.shape, _mybir.dt.from_np(a.dtype), kind="ExternalInput").ap())
    for i, (shape, dtype) in enumerate(_OUTS):
        dt = _mybir.dt.from_np(_np.dtype(dtype))
        args.append(nc.dram_tensor(f"out_{i}_dram", shape, dt, kind="ExternalOutput").ap())
    cond_resid_kernel(nc, *args)
    r = _run(nc, [arrays], core_ids=[0])
    got = tuple(r.results[0][f"out_{i}_dram"] for i in range(len(_OUTS)))
    return got[0]
```

```python
from collections import namedtuple
from contextlib import ExitStack

import concourse.bass as bass
from concourse import mybir

ALU = mybir.AluOpType
ACT = mybir.ActivationFunctionType
AX_X = mybir.AxisListType.X
F32 = mybir.dt.float32
BF16 = mybir.dt.bfloat16

P = 128
LAYERS = 3
NEG = -1e30
EPS = 1e-8
CLAMP = 256.0

LEFT_PARTS = "hhhmml"
RIGHT_PARTS = "lmhhmh"

Step = namedtuple("Step", "i par uses")


def following(s):
    return Step(s.i + 1, 1 - s.par, s.uses + s.par)


def preceding(s):
    return Step(s.i - 1, 1 - s.par, s.uses - (1 - s.par))


def wait(eng, sem, count):
    if isinstance(count, int) and count <= 0:
        return
    eng.wait_ge(sem, count)


def held(eng, *values):
    return [v if isinstance(v, int) else eng.snap(v) for v in values]


def cond_resid_kernel(nc, x, cond, ka_w, ka_b, k_w, k_b, oa_w, oa_b, o_w, o_b, w1, b1, la_w, la_b,
                      down, dgamma, dbeta, up, ugamma, ubeta, w_dec, b_dec, v_mat, out):
    B, N, F = x.shape
    S = cond.shape[1]
    H = 16
    D = F // H
    KC = F // P
    RANK = v_mat.shape[0]
    HID = down.shape[1]
    NB = 2
    T = NB * N
    STEPS = B // NB
    Q = T // P
    CH = 4
    XT = 8
    G = T // XT
    GC = G // CH
    GAIN = 1.0 / float(S) ** 0.5
    PLACED = len(LEFT_PARTS) + len(RIGHT_PARTS)
    NDEC = w_dec.shape[1]
    UCH = 16
    assert (B, N, F, S, D, KC, XT * H) == (16, 256, 256, P, 16, 2, P) and NDEC == (F + 1) * RANK

    x_rows = x.rearrange("b n f -> (b n) f")
    out_rows = out.rearrange("b n f -> (b n) f")
    rows_dram = nc.dram_tensor("rows_dram", (B, 2 * HID + 2 * F), F32, kind="Internal").ap()
    u_dram = nc.dram_tensor("u_dram", (B, UCH * 512), F32, kind="Internal").ap()
    keys_dram = nc.dram_tensor("keys_dram", (2, 4, H, 2, D, G), F32, kind="Internal").ap()

    with ExitStack() as ctx:
        def sb(name, shape, dt=F32):
            return ctx.enter_context(nc.sbuf_tensor(name, shape, dt))

        def sem(name):
            return ctx.enter_context(nc.semaphore(name))

        ident = sb("ident", [P, P])
        cond_t = sb("cond_t", [P, 32])
        table_a = sb("table_a", [P, STEPS, 8])
        table_c = sb("table_c", [P, STEPS, 17])
        cur_a = sb("cur_a", [P, 8])
        cur_c = sb("cur_c", [P, 2, 17])
        w_t = sb("w_t", [P, LAYERS, KC, F])
        down_sb = sb("down_sb", [P, KC, HID])
        up_pad = sb("up_pad", [P, NB, F])
        v_pad = sb("v_pad", [P, NB, F])
        u_all = sb("u_all", [P, B, KC, RANK])
        biases = sb("biases", [P, 9, KC])
        eps_t = sb("eps_t", [P, 96])
        b_dec_t = sb("b_dec_t", [P, KC, RANK])
        ybias = sb("ybias", [P, STEPS])
        b_dec_c = sb("b_dec_c", [P, 1])
        mask = sb("mask", [P, 2, T], BF16)
        style = sb("style", [P, 6, B])
        style2 = sb("style2", [P, 6, B])
        x_in = sb("x_in", [P, 2, Q, F])
        x_t = sb("x_t", [P, KC, T])
        x_res = sb("x_res", [P, 2, KC, T])
        keys = sb("keys", [P, KC, T])
        rest = sb("rest", [P, KC, T])
        part = {c: sb(f"part_{c}", [P, KC, T], BF16) for c in "hml"}
        gram = sb("gram", [P, 2, 2, H, T], BF16)
        keys_v = sb("keys_v", [P, 2, D, G])
        z = sb("z", [P, 2, GC, 32])
        z_t = sb("z_t", [P, 2, GC, 32])
        diag = sb("diag", [P, 2, GC, P])
        row_max = sb("row_max", [P, 2, GC])
        row_sum = sb("row_sum", [P, 2, GC])
        row_inv = sb("row_inv", [P, 2, GC])
        o_rows = sb("o_rows", [P, H, XT, GC])
        o_t = sb("o_t", [P, KC, CH, XT, GC])
        y = sb("y", [P, KC, T])
        x1 = sb("x1", [P, KC, T])
        x2 = sb("x2", [P, KC, T])
        x3 = sb("x3", [P, KC, T])
        act2 = sb("act2", [P, N])
        y3 = sb("y3", [P, N])
        out_sb = sb("out_sb", [P, Q, F])
        w_mod = [sb(f"w_mod{n}", [P, NB, KC, F]) for n in range(LAYERS)]
        down_row = sb("down_row", [P, NB, 2, HID])
        up_row = sb("up_row", [P, F])
        beta_pad = sb("beta_pad", [P, NB, F])
        w_down = sb("w_down", [P, NB, KC, HID])
        w_up_pad = sb("w_up_pad", [P, NB, F])
        u_pad = sb("u_pad", [P, NB, KC, HID])
        raw = diag[:, :, :, :].rearrange("p a g c -> p (a g c)")
        raw_w = raw[:, 0:1536].rearrange("p (l k f) -> p l k f", l=LAYERS, k=KC)
        w_sq = raw[:, 1536:3072].rearrange("p (l k f) -> p l k f", l=LAYERS, k=KC)
        raw_a = raw[:, 3072:3840].rearrange("p (l k s) -> p l k s", l=LAYERS, k=KC)
        raw_c = raw[:, 3840:3968]
        aff_t = z[:, :, :, :].rearrange("p a g c -> p (a g c)")[:, 0:768].rearrange("p (l f) -> p l f", l=LAYERS)
        gb = x3[:, :, :].rearrange("p k t -> p (k t)")
        gamma_beta = gb[:, 0:640]
        row_sb = z_t[:, :, :, :].rearrange("p a g c -> p (a g c)")[:, 0:640]
        o_w_perm = y[:, :, :].rearrange("p k t -> p (k t)")[:, 0:512].rearrange("p (o c i) -> p o c i", o=KC, c=KC)
        w_dec_sb = gram[:, 1].rearrange("p a h t -> p (a h t)").bitcast(F32)[:, 0:NDEC]
        u_sb = o_rows[:, :, :, :].rearrange("p h x g -> p (h x g)").rearrange("p (k n) -> p k n", n=512)

        psum = ctx.enter_context(nc.psum_tensor("psum", [P, 8, 512], F32))
        SC, OB, PA, PC = 0, 2, 4, 6
        pa = psum[:, PA:PA + 2, :]
        pc = psum[:, PC:PC + 2, :]

        ld_w = sem("ld_w")
        ld_dec = sem("ld_dec")
        ld_bias = sem("ld_bias")
        ld_x = [sem(f"ld_x{p}") for p in range(2)]
        st_rows = sem("st_rows")
        st_u = sem("st_u")
        ld_u = sem("ld_u")
        ld_gate = sem("ld_gate")
        st_keys = [sem(f"st_keys{p}") for p in range(2)]
        ld_keys = [sem(f"ld_keys{p}") for p in range(2)]
        ld_gram = [sem(f"ld_gram{p}") for p in range(2)]
        ld_o = sem("ld_o")
        st_out = sem("st_out")
        ident_0 = sem("ident_0")
        ident_1 = sem("ident_1")
        pads_done = sem("pads_done")
        mask_base = sem("mask_base")
        mask_done = sem("mask_done")
        ld_mask = [sem(f"ld_mask{p}") for p in range(2)]
        diag_zero = sem("diag_zero")
        su_perm = sem("su_perm")
        su_t = sem("su_t")
        su_ev = sem("su_ev")
        su_sq = sem("su_sq")
        su_style = sem("su_style")
        su_rows = sem("su_rows")
        su_rows_ev = sem("su_rows_ev")
        su_st = sem("su_st")
        su_dem = sem("su_dem")
        su_var = sem("su_var")
        su_sqrt = sem("su_sqrt")
        su_tab = sem("su_tab")
        su_u = sem("su_u")
        su_u_ev = sem("su_u_ev")
        su_o0 = sem("su_o0")
        su_uadd = sem("su_uadd")
        cur_a_set = sem("cur_a_set")
        wk_done = sem("wk_done")
        xt_mm = sem("xt_mm")
        xt_ev = sem("xt_ev")
        k_mm = sem("k_mm")
        keys_ev = sem("keys_ev")
        res_done = sem("res_done")
        h_done = sem("h_done")
        r1_done = sem("r1_done")
        m_done = sem("m_done")
        l_done = sem("l_done")
        g_mm = sem("g_mm")
        max_done = sem("max_done")
        z_done = sem("z_done")
        exp_done = sem("exp_done")
        sum_done = sem("sum_done")
        inv_done = sem("inv_done")
        norm_done = sem("norm_done")
        zt_done = sem("zt_done")
        diag_done = sem("diag_done")
        av_mm = sem("av_mm")
        o_ev = sem("o_ev")
        cur_c_set = sem("cur_c_set")
        wo_done = sem("wo_done")
        w1_done = sem("w1_done")
        gate_mul_p = sem("gate_mul_p")
        gate_mul = sem("gate_mul")
        u_done = sem("u_done")
        c1_mm = sem("c1_mm")
        x1_done = sem("x1_done")
        c2_mm = sem("c2_mm")
        c2_ev = sem("c2_ev")
        clip_done = sem("clip_done")
        x2_done = sem("x2_done")
        c3_mm = sem("c3_mm")
        act_done = sem("act_done")
        c4_mm = sem("c4_mm")
        x3_done = sem("x3_done")
        c5_mm = sem("c5_mm")
        y3_done = sem("y3_done")
        c6_mm = sem("c6_mm")
        x4_done = sem("x4_done")
        c7_mm = sem("c7_mm")
        out_ev = sem("out_ev")

        block = ctx.enter_context(nc.Block())

        def perm(ap):
            return ap.rearrange("p (a c d) -> p c d a", a=H // 2, c=KC)

        def steps(eng, body):
            body(Step(0, 0, 0), "XSB")
            body(Step(1, 1, 0), "XKSBC")
            with eng.Fori(0, (STEPS - 4) // 2) as m:
                body(Step(2 * m + 2, 0, m + 1), "XKSBC")
                body(Step(2 * m + 3, 1, m + 1), "XKSBC")
            body(Step(STEPS - 2, 0, STEPS // 2 - 1), "KSBC")
            body(Step(STEPS - 1, 1, STEPS // 2 - 1), "BC")
            body(Step(STEPS, 0, STEPS // 2), "C")

        @block.sync
        def _(sp):
            def load(dst, src, s):
                sp.dma_start(dst, src).then_inc(s, 16)

            with nc.allow_non_contiguous_dma(reason="bias columns"):
                load(raw_c[0:B, :], cond, ld_w)
                for n, w in enumerate((ka_w, oa_w, la_w)):
                    load(raw_a[:, n], w.rearrange("(k p) s -> p k s", p=P), ld_w)
                for c in range(KC):
                    load(raw_w[:, 0, c], k_w.rearrange("(a c d) i -> c d a i", a=H // 2, c=KC)[c], ld_w)
                for n, w in ((1, o_w), (2, w1)):
                    load(raw_w[:, n], w.rearrange("(k p) i -> p k i", p=P), ld_w)
                load(x_in[:, 0], x_rows[0:T, :].rearrange("(q p) f -> p q f", p=P), ld_x[0])
                for n, (v, permuted) in enumerate(((ka_b, False), (oa_b, True), (la_b, False),
                                                   (k_b, True), (o_b, False), (b1, False))):
                    for c in range(KC):
                        if permuted:
                            src = v.rearrange("(a c d) -> c d a", a=H // 2, c=KC)[c]
                        else:
                            src = v.rearrange("(c p) -> c p", c=KC)[c]
                        load(biases[:, n, c:c + 1], src, ld_bias)
                load(down_sb[:, :, :], down.rearrange("(k p) h -> p k h", p=P), ld_w)
                for n, (w, o) in enumerate(((dgamma, 0), (dbeta, HID), (ugamma, 2 * HID), (ubeta, 2 * HID + F))):
                    load(gamma_beta[:, o:o + w.shape[1]], w, ld_w)
                load(w_dec_sb, w_dec, ld_dec)
                for c in range(KC):
                    load(b_dec_t[:, c, :], b_dec[c * P * RANK:(c + 1) * P * RANK].rearrange("(p k) -> p k", k=RANK), ld_dec)
                sp.wait_ge(pads_done, 7)
                for b in range(NB):
                    load(up_pad[HID * b:HID * (b + 1), b, :], up, ld_dec)
                    load(v_pad[64 * b:64 * b + RANK, b, :], v_mat, ld_dec)
                    load(b_dec_c[64 * b:64 * b + RANK, :], b_dec[F * RANK:(F + 1) * RANK].rearrange("(k o) -> k o", o=1), ld_dec)
                sp.wait_ge(su_rows_ev, 2)
                sp.dma_start(rows_dram, row_sb[0:B, :]).then_inc(st_rows, 16)

            def decoder_out():
                sp.wait_ge(su_u_ev, 3)
                for c in range(4):
                    dst = u_dram.rearrange("b (k c n) -> c b k n", c=4, n=512)[c]
                    if c < 3:
                        sp.dma_start(dst, u_sb[32 * c:32 * c + B, :, :]).then_inc(st_u, 16)
                    else:
                        sp.dma_start(dst[:, 0:3, :], u_sb[96:96 + B, 0:3, :]).then_inc(st_u, 16)
                        last = NDEC - (UCH - 1) * 512
                        sp.dma_start(dst[:, 3, 0:last], u_sb[96:96 + B, 3, 0:last]).then_inc(st_u, 16)
                sp.wait_ge(st_u, 16 * 5)
                with nc.allow_non_contiguous_dma(reason="bias columns"):
                    for c in range(KC):
                        src = u_dram[:, c * P * RANK:(c + 1) * P * RANK].rearrange("b (p k) -> p b k", k=RANK)
                        sp.dma_start(u_all[:, :, c, :], src).then_inc(ld_u, 16)
                    for b in range(NB):
                        src = u_dram.rearrange("(s b) n -> b n s", b=NB)[b][F * RANK:(F + 1) * RANK, :]
                        sp.dma_start(ybias[64 * b:64 * b + RANK, :], src).then_inc(ld_u, 16)

            def gates(s):
                used, first = held(sp, 2 * s.i, NB * s.i)
                rows = rows_dram[bass.ds(first, NB), :]
                wait(sp, gate_mul, used)
                sp.dma_start(down_row[:, :, :, :].rearrange("p b a h -> p b (a h)"),
                             rows[:, 0:2 * HID].unsqueeze(0).to_broadcast([P, NB, 2 * HID])).then_inc(ld_gate, 16)
                gamma, beta = rows[:, 2 * HID:2 * HID + F], rows[:, 2 * HID + F:2 * HID + 2 * F]
                sp.dma_start(up_row[:, :], gamma.unsqueeze(1).to_broadcast([NB, HID, F])).then_inc(ld_gate, 16)
                for b in range(NB):
                    sp.dma_start(beta_pad[HID * b:HID * (b + 1), b, :], beta[b:b + 1, :].to_broadcast([HID, F]))\
                        .then_inc(ld_gate, 16)

            def mask_rows(par):
                for side in range(2):
                    sp.dma_start(gram[96:98, par, side],
                                 mask[96:98, side, :].unsqueeze(1).to_broadcast([2, H, T]))\
                        .then_inc(ld_mask[par], 16)

            def spread(a):
                evacuated, read, split, stored = held(sp, 4 * (a.i + 1), CH * (a.i - 1), a.i + 1, 64 * (a.uses + 1))
                sp.wait_ge(keys_ev, evacuated)
                for q in range(4):
                    sp.dma_start(keys_dram[a.par, q].rearrange("j t d g -> d (j t) g"),
                                 keys[:, :, :].rearrange("p b (t q g) -> p (b t) q g", t=2, q=4)[:, :, q, :])\
                        .then_inc(st_keys[a.par], 16)
                wait(sp, g_mm, read)
                if isinstance(a.i, int) and a.i == 1:
                    sp.wait_ge(su_u, UCH)
                    mask_rows(1)
                for c, done in (("h", h_done), ("m", m_done), ("l", l_done)):
                    sp.wait_ge(done, split)
                    for side, order in enumerate((LEFT_PARTS, RIGHT_PARTS)):
                        for g, o in enumerate(order):
                            if o == c:
                                sp.dma_start(gram[16 * g:16 * g + 16, a.par, side, :, :], part[c][:, :, :])\
                                    .then_inc(ld_gram[a.par], 16)
                sp.wait_ge(st_keys[a.par], stored)
                wait(sp, av_mm, read)
                sp.dma_start(keys_v[:, a.par, :, :], keys_dram[a.par].rearrange("q j t d g -> (q j t) d g"))\
                    .then_inc(ld_keys[a.par], 16)

            def load_x(a):
                first, used = held(sp, a.i * T, 2 * (a.i - 1))
                rows = x_rows[bass.ds(first, T), :].rearrange("(q p) f -> p q f", p=P)
                wait(sp, xt_mm, used)
                sp.dma_start(x_in[:, a.par], rows).then_inc(ld_x[a.par], 16)

            def body(s, stages):
                if "X" in stages:
                    load_x(following(following(s)))
                if "K" in stages:
                    spread(following(s))
                if "B" in stages:
                    sp.wait_ge(o_ev, CH * (s.i + 1))
                    for t in range(CH):
                        sp.dma_start(o_t[:, :, t].rearrange("p k x g -> p k (x g)"),
                                     o_rows[32 * t:32 * t + D].rearrange("p h x g -> p h (x g)")).then_inc(ld_o, 16)
                    gates(s)
                if "C" in stages:
                    c = preceding(s)
                    first, ready = held(sp, c.i * T, 2 * (c.i + 1))
                    rows = out_rows[bass.ds(first, T), :].rearrange("(q p) f -> p q f", p=P)
                    sp.wait_ge(out_ev, ready)
                    sp.dma_start(rows, out_sb[:, :, :]).then_inc(st_out, 16)

            sp.wait_ge(mask_done, 2)
            mask_rows(0)
            load_x(Step(1, 1, 0))
            spread(Step(0, 0, 0))
            decoder_out()
            spread(Step(1, 1, 0))
            sp.wait_ge(st_rows, 16)
            steps(sp, body)
            sp.wait_ge(st_out, 16 * STEPS)

        @block.gpsimd
        def _(pool):
            pool.memset(ident[:, :], 0.0).then_inc(ident_0, 1)
            pool.wait_ge(ident_0, 1)
            pool.affine_select(out=ident[:, :], in_=ident[:, :], compare_op=ALU.not_equal, fill=1.0,
                               base=0, pattern=[[-1, P]], channel_multiplier=1).then_inc(ident_1, 1)
            pool.memset(cond_t[:, :], 0.0).then_inc(pads_done, 1)
            pool.memset(v_pad[:, :, :], 0.0).then_inc(pads_done, 1)
            pool.memset(b_dec_c[:, :], 0.0).then_inc(pads_done, 1)
            pool.memset(ybias[:, :], 0.0).then_inc(pads_done, 1)
            pool.memset(u_pad[:, :, :, :], 0.0).then_inc(pads_done, 1)
            pool.memset(beta_pad[:, :, :], 0.0).then_inc(pads_done, 1)
            pool.memset(up_pad[:, :, :], 0.0).then_inc(pads_done, 1)

            left, right = (mask[96:98, side, :].rearrange("p (t g) -> p t g", t=2) for side in range(2))
            pool.wait_ge(pads_done, 7)
            pool.memset(left, 1.0).then_inc(mask_base, 1)
            pool.memset(right, 0.0).then_inc(mask_base, 1)
            pool.wait_ge(mask_base, 2)
            for ap, fill in ((left, 0.0), (right, NEG)):
                pool.affine_select(out=ap, in_=ap, compare_op=ALU.is_equal, fill=fill, base=0,
                                   pattern=[[-1, 2], [0, N]], channel_multiplier=1).then_inc(mask_done, 1)
            pool.wait_ge(mask_done, 2)
            pool.wait_ge(su_dem, 1)
            pool.memset(diag[:, :, :, :], 0.0).then_inc(diag_zero, 1)

            def normalise(s, n):
                pool.wait_ge(inv_done, CH * s.i + n + 1)
                pool.wait_ge(exp_done, CH * s.i + n + 1)
                b = n % 2
                pool.tensor_tensor(z[:, b], z[:, b], row_inv[:, b, :].unsqueeze(2).to_broadcast([P, GC, 32]),
                                   ALU.mult).then_inc(norm_done, 1)

            def residue(a):
                pool.wait_ge(h_done, a.i + 1)
                wait(pool, l_done, a.i)
                pool.tensor_tensor(rest[:, :, :], keys[:, :, :], part["h"][:, :, :], ALU.subtract)\
                    .then_inc(r1_done, 1)

            def modulate(n, c, col, done):
                styles = cur_c[:, c.par, col:col + 4].rearrange("p (k b) -> p b k", b=NB)
                pool.tensor_tensor(w_mod[n][:, :, :, :], w_t[:, n].unsqueeze(1).to_broadcast([P, NB, KC, F]),
                                   styles.unsqueeze(3).to_broadcast([P, NB, KC, F]), ALU.mult).then_inc(done, 1)

            def modulate_low_rank(c):
                pool.wait_ge(ld_gate, 64 * (c.i + 1))
                wait(pool, c4_mm, 2 * c.i)
                for b in range(NB):
                    gam = down_row[:, b, 0, :].unsqueeze(1).to_broadcast([P, KC, HID])
                    pool.tensor_tensor(w_down[:, b], down_sb[:, :, :], gam, ALU.mult).then_inc(gate_mul_p, 1)
                pool.tensor_tensor(w_up_pad[:, :, :], up_pad[:, :, :],
                                   up_row[:, :].unsqueeze(1).to_broadcast([P, NB, F]), ALU.mult)\
                    .then_inc(gate_mul_p, 1)
                pool.wait_ge(gate_mul_p, 3 * (c.i + 1))
                for b in range(NB):
                    beta = down_row[:, b, 1, :].unsqueeze(1).to_broadcast([P, KC, HID])
                    mul = pool.tensor_tensor(w_down[:, b], w_down[:, b], beta, ALU.add)
                mul.then_inc(gate_mul, 1)
                pool.tensor_tensor(w_up_pad[:, :, :], w_up_pad[:, :, :], beta_pad[:, :, :], ALU.add)\
                    .then_inc(gate_mul, 1)

            def body(s, stages):
                c = preceding(s)
                if "B" in stages:
                    normalise(s, 0)
                    normalise(s, 1)
                if isinstance(s.i, int) and s.i == 0:
                    pool.wait_ge(ld_u, 64)
                    pool.wait_ge(ld_dec, 16 * 9)
                    pool.tensor_tensor(table_c[:, :, 16], ybias[:, :], b_dec_c[:, :].to_broadcast([P, STEPS]),
                                       ALU.add).then_inc(su_uadd, 1)
                    pool.tensor_tensor(u_all[:, :, :, :], u_all[:, :, :, :],
                                       b_dec_t[:, :, :].rearrange("p c k -> p (c k)").unsqueeze(1)
                                       .to_broadcast([P, B, KC * RANK]).rearrange("p b (c k) -> p b c k", c=KC),
                                       ALU.add).then_inc(su_uadd, 1)
                if "C" in stages:
                    modulate_low_rank(c)
                if "B" in stages:
                    normalise(s, 2)
                    normalise(s, 3)
                if "K" in stages:
                    residue(following(s))
                if "B" in stages:
                    pool.wait_ge(cur_c_set, s.i + 1)
                    wait(pool, c1_mm, 2 * s.i)
                    modulate(1, s, 0, wo_done)
                    wait(pool, c2_mm, 2 * s.i)
                    modulate(2, s, 8, w1_done)

            residue(Step(0, 0, 0))
            residue(Step(1, 1, 0))
            steps(pool, body)

        @block.scalar
        def _(act):
            for n in range(LAYERS):
                act.wait_ge(su_t, 3 + n)
                act.activation(w_t[:, n].rearrange("p k f -> p (k f)"), psum[:, 2 + n, :], ACT.Copy)\
                    .then_inc(su_ev, 1)
                act.activation(w_sq[:, n].rearrange("p k f -> p (k f)"), psum[:, 2 + n, :], ACT.Square)\
                    .then_inc(su_sq, 1)
            act.wait_ge(su_rows, 1)
            act.activation(row_sb[0:32, 0:2 * HID], psum[0:32, 7, 0:2 * HID], ACT.Copy).then_inc(su_rows_ev, 1)
            act.activation(row_sb[0:32, 2 * HID:640], psum[0:32, 6, :], ACT.Copy).then_inc(su_rows_ev, 1)
            act.wait_ge(su_var, 1)
            act.activation(eps_t[:, :], eps_t[:, :], ACT.Sqrt).then_inc(su_sqrt, 1)

            def x_evacuate(a):
                act.wait_ge(xt_mm, 2 * (a.i + 1))
                wait(act, k_mm, 2 * a.i)
                wait(act, res_done, 2 * a.i)
                act.activation(x_t[:, :, :], pa, ACT.Copy).then_inc(xt_ev, 1)

            def keys_evacuate(a):
                if isinstance(a.i, int) and a.i == 0:
                    act.wait_ge(ld_bias, 16 * 12)
                else:
                    before = preceding(a)
                    act.wait_ge(st_keys[before.par], 64 * (before.uses + 1))
                    act.wait_ge(r1_done, a.i)
                    act.wait_ge(h_done, a.i)
                act.wait_ge(cur_a_set, a.i + 1)
                for c in range(KC):
                    act.wait_ge(k_mm, 2 * a.i + c + 1)
                    for b in range(NB):
                        t = slice(N * b, N * (b + 1))
                        act.activation(keys[:, c, t], pa[:, c, t], ACT.Identity, bias=biases[:, 3, c:c + 1],
                                       scale=cur_a[:, 4 + 2 * c + b:5 + 2 * c + b]).then_inc(keys_ev, 1)

            def exponent(s, n):
                act.wait_ge(z_done, CH * s.i + n + 1)
                b = n % 2
                act.activation(z[:, b], z[:, b], ACT.Exp, scale=D ** -0.5).then_inc(exp_done, 1)

            def spread_diagonal(s, n):
                act.wait_ge(zt_done, CH * s.i + n + 1)
                wait(act, av_mm, CH * s.i + n - 1)
                if isinstance(s.i, int) and s.i == 0 and n == 0:
                    act.wait_ge(diag_zero, 1)
                b = n % 2
                for q in range(4):
                    r = slice(32 * q, 32 * q + 32)
                    act.activation(diag[r, b, :, r], z_t[r, b], ACT.Copy).then_inc(diag_done, 1)

            def body(s, stages):
                c = preceding(s)
                if "B" in stages:
                    exponent(s, 1)
                    spread_diagonal(s, 0)
                    spread_diagonal(s, 1)
                    exponent(s, 2)
                    exponent(s, 3)
                if "K" in stages:
                    keys_evacuate(following(s))
                if "C" in stages:
                    act.wait_ge(cur_c_set, c.i + 1)
                    wait(act, x2_done, 2 * c.i)
                    for o in range(KC):
                        act.wait_ge(c2_mm, 2 * c.i + o + 1)
                        for b in range(NB):
                            t = slice(N * b, N * (b + 1))
                            k = 12 + 2 * o + b
                            act.activation(y[:, o, t], pc[:, o, t], ACT.Identity, bias=biases[:, 5, o:o + 1],
                                           scale=cur_c[:, c.par, k:k + 1]).then_inc(c2_ev, 1)
                if "B" in stages:
                    spread_diagonal(s, 2)
                if "C" in stages:
                    act.wait_ge(c3_mm, c.i + 1)
                    wait(act, c4_mm, 2 * c.i)
                    act.activation(act2[:, :], pc[:, 0, 0:N], ACT.Relu).then_inc(act_done, 1)
                if "B" in stages:
                    spread_diagonal(s, 3)
                if "C" in stages:
                    act.wait_ge(c5_mm, c.i + 1)
                    wait(act, c6_mm, 2 * c.i)
                    act.activation(y3[:, :], pc[:, 0, 0:N], ACT.Identity, bias=cur_c[:, c.par, 16:17])\
                        .then_inc(y3_done, 1)
                if "X" in stages:
                    x_evacuate(following(following(s)))
                if "C" in stages:
                    wait(act, st_out, 16 * c.i)
                    for o in range(2):
                        act.wait_ge(c7_mm, 2 * c.i + o + 1)
                        act.activation(out_sb[:, 2 * o:2 * o + 2, :].rearrange("p q f -> p (q f)"), pc[:, o, :],
                                       ACT.Copy).then_inc(out_ev, 1)
                if "S" in stages:
                    exponent(following(s), 0)

            x_evacuate(Step(0, 0, 0))
            keys_evacuate(Step(0, 0, 0))
            x_evacuate(Step(1, 1, 0))
            keys_evacuate(Step(1, 1, 0))
            exponent(Step(0, 0, 0), 0)
            steps(act, body)

        @block.vector
        def _(dve):
            dve.wait_ge(ld_w, 16 * 13)
            for o in range(KC):
                dve.tensor_copy(o_w_perm[:, o].rearrange("p c (d a) -> p c d a", d=D), perm(raw_w[:, 1, o, :]))\
                    .then_inc(su_perm, 1)
            dve.wait_ge(su_t, 2)
            dve.wait_ge(pads_done, 7)
            flat = psum[:, 0:2, :].rearrange("p k n -> p (k n)")
            dve.tensor_copy(aff_t[:, 0, :], flat[:, 0:F]).then_inc(su_ev, 1)
            dve.tensor_copy(aff_t[:, 1, :].rearrange("p (c d a) -> p c d a", c=KC, d=D), perm(flat[:, F:2 * F]))\
                .then_inc(su_ev, 1)
            dve.tensor_scalar(aff_t[:, 2, :], flat[:, 2 * F:3 * F], GAIN, None, ALU.mult).then_inc(su_ev, 1)
            dve.tensor_copy(cond_t[:, 0:B], flat[:, 3 * F:3 * F + B]).then_inc(su_ev, 1)
            dve.wait_ge(su_style, 1)
            dve.wait_ge(ld_bias, 16 * 12)
            dve.tensor_tensor(style[:, :, :], psum[:, 5, 0:96].rearrange("p (k b) -> p k b", b=B),
                              biases[:, 0:3, :].rearrange("p l c -> p (l c)").unsqueeze(2).to_broadcast([P, 6, B]),
                              ALU.add).then_inc(su_st, 1)
            dve.wait_ge(su_st, 1)
            dve.tensor_tensor(style2[:, :, :], style[:, :, :], style[:, :, :], ALU.mult).then_inc(su_st, 1)

            def by_step(ap):
                return ap.rearrange("p c (s b) -> p c s b", b=NB)

            def columns(table, at):
                return table[:, :, at:at + 4].rearrange("p s (c b) -> p c s b", b=NB)

            dve.tensor_copy(columns(table_a, 0), by_step(style[:, 0:2, :])).then_inc(su_tab, 1)
            dve.tensor_copy(columns(table_c, 0), by_step(style[:, 2:4, :])).then_inc(su_tab, 1)
            dve.tensor_copy(columns(table_c, 8), by_step(style[:, 4:6, :])).then_inc(su_tab, 1)
            dve.wait_ge(su_dem, 1)
            dve.tensor_scalar(eps_t[:, :], psum[:, 0, 0:96], EPS, None, ALU.add).then_inc(su_var, 1)
            dve.wait_ge(su_sqrt, 1)
            dem = style2[:, :, :].rearrange("p k b -> p (k b)")
            dve.reciprocal(dem, eps_t[:, :]).then_inc(su_st, 1)
            dve.wait_ge(su_st, 3)
            dve.tensor_copy(columns(table_a, 4), by_step(style2[:, 0:2, :])).then_inc(su_tab, 1)
            dve.tensor_copy(columns(table_c, 4), by_step(style2[:, 2:4, :])).then_inc(su_tab, 1)
            dve.tensor_copy(columns(table_c, 12), by_step(style2[:, 4:6, :])).then_inc(su_tab, 1)

            def prepare_a(a):
                wait(dve, keys_ev, 4 * a.i)
                dve.tensor_copy(cur_a[:, :], table_a[:, a.i, :]).then_inc(cur_a_set, 1)
                dve.wait_ge(cur_a_set, a.i + 1)
                wait(dve, k_mm, 2 * a.i)
                for b in range(NB):
                    for c in range(KC):
                        dve.tensor_scalar(w_mod[0][:, b, c, :], w_t[:, 0, c, :],
                                          cur_a[:, 2 * c + b:2 * c + b + 1], None, ALU.mult).then_inc(wk_done, 1)

            def keep_x(a):
                dve.wait_ge(xt_ev, a.i + 1)
                for c in range(KC):
                    dve.tensor_scalar(x_res[:, a.par, c, :], x_t[:, c, :], biases[:, 4, c:c + 1], None, ALU.add)\
                        .then_inc(res_done, 1)

            def split_high(a):
                dve.wait_ge(keys_ev, 4 * (a.i + 1))
                if not (isinstance(a.i, int) and a.i == 0):
                    before = preceding(a)
                    dve.wait_ge(ld_gram[before.par], 16 * PLACED * (before.uses + 1))
                dve.tensor_copy(part["h"][:, :, :], keys[:, :, :]).then_inc(h_done, 1)

            def split_low(a):
                dve.wait_ge(r1_done, a.i + 1)
                dve.tensor_copy(part["m"][:, :, :], rest[:, :, :]).then_inc(m_done, 1)
                dve.wait_ge(m_done, a.i + 1)
                dve.tensor_tensor(part["l"][:, :, :], rest[:, :, :], part["m"][:, :, :], ALU.subtract)\
                    .then_inc(l_done, 1)

            def shift(s, n):
                k = CH * s.i + n
                b = n % 2
                dve.wait_ge(g_mm, k + 1)
                scores = psum[:, SC + b, :].rearrange("p (g j) -> p g j", j=32)
                dve.tensor_reduce(row_max[:, b, :], scores, AX_X, ALU.max).then_inc(max_done, 1)
                dve.wait_ge(max_done, k + 1)
                wait(dve, zt_done, k - 1)
                dve.tensor_tensor(z[:, b], scores, row_max[:, b, :].unsqueeze(2).to_broadcast([P, GC, 32]),
                                  ALU.subtract).then_inc(z_done, 1)

            def row_sums(s, n):
                k = CH * s.i + n
                b = n % 2
                dve.wait_ge(exp_done, k + 1)
                dve.tensor_reduce(row_sum[:, b, :], z[:, b], AX_X, ALU.add).then_inc(sum_done, 1)
                dve.wait_ge(sum_done, k + 1)
                wait(dve, norm_done, k - 1)
                dve.reciprocal(row_inv[:, b, :], row_sum[:, b, :]).then_inc(inv_done, 1)

            def transpose(s, n):
                k = CH * s.i + n
                b = n % 2
                dve.wait_ge(norm_done, k + 1)
                wait(dve, diag_done, 4 * (k - 1))
                dve.transpose(z_t[:, b].rearrange("p g j -> p (g j)"), z[:, b].rearrange("p g j -> p (g j)"))\
                    .then_inc(zt_done, 1)

            def o_evacuate(s, n):
                k = CH * s.i + n
                dve.wait_ge(av_mm, k + 1)
                if n == 0:
                    wait(dve, ld_o, 64 * s.i)
                    if isinstance(s.i, int) and s.i == 0:
                        dve.wait_ge(st_u, 16 * 5)
                src = psum[:, OB + n % 2, :].rearrange("p (r q h) -> p r q h", r=4, q=4)
                dst = o_rows[:, :, :, n * 4:n * 4 + 4].rearrange("p h (t q) r -> p r q (h t)", t=2)
                dve.tensor_copy(dst, src).then_inc(o_ev, 1)

            def add_l0(c, o):
                dve.wait_ge(c1_mm, 2 * c.i + o + 1)
                for b in range(NB):
                    t = slice(N * b, N * (b + 1))
                    k = 4 + 2 * o + b
                    last = dve.scalar_tensor_tensor(x1[:, o, t], pc[:, o, t], cur_c[:, c.par, k:k + 1],
                                                    x_res[:, c.par, o, t], ALU.mult, ALU.add)
                last.then_inc(x1_done, 1)

            def clip(c, o):
                dve.wait_ge(c2_ev, 4 * c.i + 2 * o + 2)
                dve.tensor_scalar(y[:, o, :], y[:, o, :], -CLAMP, CLAMP, ALU.max, ALU.min).then_inc(clip_done, 1)

            def body(s, stages):
                c = preceding(s)
                a = following(s)
                if "C" in stages:
                    dve.wait_ge(cur_c_set, c.i + 1)
                    dve.wait_ge(res_done, 2 * (c.i + 1))
                    wait(dve, x2_done, 2 * c.i)
                    add_l0(c, 0)
                if "B" in stages:
                    transpose(s, 0)
                    row_sums(s, 1)
                if "C" in stages:
                    add_l0(c, 1)
                if "B" in stages:
                    transpose(s, 1)
                    shift(s, 2)
                    shift(s, 3)
                    row_sums(s, 2)
                    row_sums(s, 3)
                if "K" in stages:
                    keep_x(a)
                if "B" in stages:
                    transpose(s, 2)
                if "K" in stages:
                    split_high(a)
                if "B" in stages:
                    transpose(s, 3)
                if "C" in stages:
                    clip(c, 0)
                    clip(c, 1)
                    for o in range(KC):
                        dve.wait_ge(clip_done, 2 * c.i + o + 1)
                        dve.tensor_tensor(x2[:, o, :], y[:, o, :], x1[:, o, :], ALU.add).then_inc(x2_done, 1)
                if "B" in stages:
                    o_evacuate(s, 0)
                    o_evacuate(s, 1)
                if "K" in stages:
                    split_low(a)
                if "B" in stages:
                    if isinstance(s.i, int) and s.i == 0:
                        dve.wait_ge(su_uadd, 1)
                    wait(dve, y3_done, s.i - 1)
                    dve.tensor_copy(cur_c[:, s.par], table_c[:, s.i, :]).then_inc(cur_c_set, 1)
                    o_evacuate(s, 2)
                if "C" in stages:
                    wait(dve, c7_mm, 2 * c.i)
                    for o in range(KC):
                        dve.wait_ge(c4_mm, 2 * c.i + o + 1)
                        dve.scalar_tensor_tensor(x3[:, o, :], x2[:, o, :], 2.0, pc[:, o, :], ALU.mult, ALU.add)\
                            .then_inc(x3_done, 1)
                if "X" in stages:
                    prepare_a(following(a))
                if "B" in stages:
                    o_evacuate(s, 3)
                    if isinstance(s.i, int) and s.i == 0:
                        dve.wait_ge(su_uadd, 2)
                    wait(dve, c5_mm, s.i)
                    dve.tensor_copy(u_pad[:, :, :, 0:RANK], u_all[:, bass.ds(NB * s.i, NB), :, :])\
                        .then_inc(u_done, 1)
                if "C" in stages:
                    for o in range(KC):
                        dve.wait_ge(c6_mm, 2 * c.i + o + 1)
                        dve.tensor_tensor(x3[:, o, :], pc[:, o, :], x3[:, o, :], ALU.add).then_inc(x4_done, 1)
                if "S" in stages:
                    shift(a, 0)
                    row_sums(a, 0)
                    shift(a, 1)

            dve.wait_ge(su_tab, 6)
            first = Step(0, 0, 0)
            prepare_a(first)
            keep_x(first)
            split_high(first)
            split_low(first)
            prepare_a(following(first))
            dve.wait_ge(su_u, UCH)
            dve.tensor_copy(u_sb[:, 0:3, :], psum[:, 0:3, :]).then_inc(su_u_ev, 1)
            dve.tensor_copy(u_sb[0:96, 3, :], psum[0:96, 3, :]).then_inc(su_u_ev, 1)
            last = NDEC - (UCH - 1) * 512
            dve.tensor_copy(u_sb[96:128, 3, 0:last], psum[96:128, 3, 0:last]).then_inc(su_u_ev, 1)
            dve.wait_ge(su_u_ev, 3)
            dve.memset(psum[:, OB:OB + 2, :], 0.0).then_inc(su_o0, 1)
            shift(first, 0)
            row_sums(first, 0)
            shift(first, 1)
            keep_x(following(first))
            split_high(following(first))
            split_low(following(first))
            steps(dve, body)

        @block.tensor
        def _(pe):
            mm = nc.tensor.matmul
            pe.wait_ge(ident_1, 1)
            pe.wait_ge(ld_w, 16 * 13)
            slot = psum[:, 0:5, :].rearrange("p k (s n) -> p (k s) n", n=P)
            for n in range(LAYERS):
                for c in range(KC):
                    last = nc.tensor.transpose(slot[:, 2 * n + c, :], raw_a[:, n, c, :], ident[:, :])
                    if 2 * n + c == 3:
                        last.then_inc(su_t, 1)
            nc.tensor.transpose(slot[:, 6, 0:B], raw_c[0:B, :], ident[0:B, 0:B]).then_inc(su_t, 1)
            pe.wait_ge(su_perm, 2)
            for n in range(LAYERS):
                for c in range(KC):
                    for o in range(KC):
                        src = raw_w[:, n, o, :]
                        src = o_w_perm[:, o, c, :] if n == 1 else src[:, c * P:(c + 1) * P]
                        last = nc.tensor.transpose(slot[:, 8 + 4 * n + 2 * c + o, :], src, ident[:, :])
                last.then_inc(su_t, 1)
            pe.wait_ge(su_ev, 7)
            for n in range(LAYERS):
                for c in range(KC):
                    src = aff_t[:, n, c * P:(c + 1) * P]
                    k = (2 * n + c) * B
                    last = mm(psum[:, 5, k:k + B], src, cond_t[:, 0:B], start=True, stop=True)
            last.then_inc(su_style, 1)
            mm(psum[0:32, 7, 0:2 * HID], cond_t[:, :], gamma_beta[:, 0:2 * HID], start=True, stop=True)
            mm(psum[0:32, 6, :], cond_t[:, :], gamma_beta[:, 2 * HID:640], start=True, stop=True).then_inc(su_rows, 1)
            pe.wait_ge(su_st, 2)
            pe.wait_ge(su_sq, LAYERS)
            for n in range(LAYERS):
                for o in range(KC):
                    k = (2 * n + o) * B
                    for c in range(KC):
                        last = mm(psum[:, 0, k:k + B], w_sq[:, n, c, o * P:(o + 1) * P], style2[:, 2 * n + c, :],
                                  start=(c == 0), stop=(c == KC - 1))
            last.then_inc(su_dem, 1)

            def x_transposes(a):
                pe.wait_ge(ld_x[a.par], 16 * (a.uses + 1))
                wait(pe, keys_ev, 4 * a.i)
                for c in range(KC):
                    for q in range(Q):
                        last = nc.tensor.transpose(pa[:, c, q * P:(q + 1) * P],
                                                   x_in[:, a.par, q, c * P:(c + 1) * P], ident[:, :])
                    last.then_inc(xt_mm, 1)

            def project_keys(a):
                pe.wait_ge(xt_ev, a.i + 1)
                pe.wait_ge(wk_done, 4 * (a.i + 1))
                for o in range(KC):
                    for b in range(NB):
                        for c in range(KC):
                            last = mm(pa[:, o, N * b:N * (b + 1)], w_mod[0][:, b, c, o * P:(o + 1) * P],
                                      x_t[:, c, N * b:N * (b + 1)], start=(c == 0), stop=(c == KC - 1))
                    last.then_inc(k_mm, 1)

            def decoder():
                pe.wait_ge(ld_dec, 16 * 9)
                pe.wait_ge(su_var, 1)
                for k in range(UCH):
                    q = k % 4
                    w = min(512, NDEC - 512 * k)
                    mm(psum[32 * q:32 * q + 32, k // 4, 0:w], cond_t[:, :], w_dec_sb[:, 512 * k:512 * k + w],
                       start=True, stop=True).then_inc(su_u, 1)

            def scores(s, n):
                if n == 0:
                    pe.wait_ge(ld_gram[s.par], 16 * PLACED * (s.uses + 1))
                if isinstance(s.i, int) and s.i == 0 and n == 0:
                    pe.wait_ge(ld_mask[0], 32)
                    pe.wait_ge(su_u_ev, 3)
                wait(pe, z_done, CH * s.i + n - 1)
                left, right = (gram[0:98, s.par, side].rearrange("p h (t m) -> p (h t) m", t=2) for side in range(2))
                for g in range(GC):
                    grp = (g // 4) * GC + n * 4 + g % 4
                    for q in range(4):
                        last = mm(psum[32 * q:32 * q + 32, SC + n % 2, 32 * g:32 * g + 32],
                                  left[:, :, q * G + grp], right[:, :, q * G + grp],
                                  start=True, stop=True)
                last.then_inc(g_mm, 1)

            def values(s, n):
                if n == 0:
                    pe.wait_ge(ld_keys[s.par], 16 * (s.uses + 1))
                    if isinstance(s.i, int) and s.i == 0:
                        pe.wait_ge(su_o0, 1)
                k = CH * s.i + n
                pe.wait_ge(diag_done, 4 * (k + 1))
                wait(pe, o_ev, k - 1)
                for r in range(4):
                    for c in range(4):
                        last = mm(psum[32 * c:32 * c + D, OB + n % 2, P * r:P * (r + 1)],
                                  keys_v[:, s.par, :, c * GC + n * 4 + r], diag[:, n % 2, c * 4 + r, :],
                                  start=True, stop=True)
                last.then_inc(av_mm, 1)

            def project_o(c):
                pe.wait_ge(ld_o, 64 * (c.i + 1))
                pe.wait_ge(wo_done, c.i + 1)
                wait(pe, out_ev, 2 * c.i)
                for o in range(KC):
                    for b in range(NB):
                        for k in range(KC):
                            src = o_t[:, k, :, 4 * b:4 * b + 4, :].rearrange("p c x g -> p x c g")
                            last = mm(pc[:, o, N * b:N * (b + 1)], w_mod[1][:, b, k, o * P:(o + 1) * P], src,
                                      start=(k == 0), stop=(k == KC - 1))
                    last.then_inc(c1_mm, 1)

            def layer1(c):
                pe.wait_ge(x1_done, 2 * (c.i + 1))
                pe.wait_ge(w1_done, c.i + 1)
                for o in range(KC):
                    for b in range(NB):
                        for k in range(KC):
                            last = mm(pc[:, o, N * b:N * (b + 1)], w_mod[2][:, b, k, o * P:(o + 1) * P],
                                      x1[:, k, N * b:N * (b + 1)], start=(k == 0), stop=(k == KC - 1))
                    last.then_inc(c2_mm, 1)

            def low_rank_in(w, src, done):
                for k in range(KC):
                    for b in range(NB):
                        last = mm(pc[64 * b:64 * b + 64, 0, 0:N], w[:, b, k, :], src[:, k, N * b:N * (b + 1)],
                                  start=(k == 0), stop=(k == KC - 1))
                last.then_inc(done, 1)

            def low_rank_out(w, src, done):
                for o in range(KC):
                    for b in range(NB):
                        last = mm(pc[:, o, N * b:N * (b + 1)], w[:, b, o * P:(o + 1) * P], src[:, :],
                                  start=True, stop=True)
                    last.then_inc(done, 1)

            def body(s, stages):
                c, a = preceding(s), following(s)
                attention, rest = "B" in stages, "C" in stages
                if rest:
                    project_o(c)
                if attention:
                    scores(s, 2)
                    scores(s, 3)
                if "K" in stages:
                    project_keys(a)
                if rest:
                    layer1(c)
                if attention:
                    values(s, 0)
                    values(s, 1)
                if rest:
                    pe.wait_ge(x2_done, 2 * (c.i + 1))
                    pe.wait_ge(gate_mul, 2 * (c.i + 1))
                    low_rank_in(w_down, x2, c3_mm)
                if attention:
                    values(s, 2)
                if rest:
                    pe.wait_ge(act_done, c.i + 1)
                    low_rank_out(w_up_pad, act2, c4_mm)
                if attention:
                    values(s, 3)
                if rest:
                    pe.wait_ge(x3_done, 2 * (c.i + 1))
                    pe.wait_ge(u_done, c.i + 1)
                    low_rank_in(u_pad, x3, c5_mm)
                if "X" in stages:
                    x_transposes(following(a))
                if rest:
                    pe.wait_ge(y3_done, c.i + 1)
                    low_rank_out(v_pad, y3, c6_mm)
                if isinstance(s.i, int) and s.i == 0:
                    pe.wait_ge(ld_mask[1], 32)
                if "S" in stages:
                    scores(a, 0)
                if rest:
                    pe.wait_ge(x4_done, 2 * (c.i + 1))
                    for o in range(2):
                        for q in range(2 * o, 2 * o + 2):
                            for k in range(KC):
                                at = (q % 2) * F + k * P
                                last = nc.tensor.transpose(pc[:, o, at:at + P], x3[:, k, q * P:(q + 1) * P],
                                                           ident[:, :])
                        last.then_inc(c7_mm, 1)
                if "S" in stages:
                    scores(a, 1)

            first = Step(0, 0, 0)
            x_transposes(first)
            project_keys(first)
            x_transposes(following(first))
            decoder()
            project_keys(following(first))
            scores(first, 0)
            scores(first, 1)
            steps(pe, body)


_INS = ['x', 'cond_512', 'L0_cond_k_aff_w', 'L0_cond_k_aff_b', 'L0_cond_k_w', 'L0_cond_k_b', 'L0_cond_o_aff_w',
        'L0_cond_o_aff_b', 'L0_cond_o_w', 'L0_cond_o_b', 'L1_cond_weight', 'L1_cond_bias', 'L1_cond_affine_w',
        'L1_cond_affine_b', 'L2_cond_down_project', 'L2_cond_down_gamma', 'L2_cond_down_beta',
        'L2_cond_up_project', 'L2_cond_up_gamma', 'L2_cond_up_beta', 'L3_cond_W_dec', 'L3_cond_b_dec', 'L3_cond_V']
_OUTS = [((16, 256, 256), 'float32')]


def kernel(**inputs):
    import numpy as _np
    import concourse.bacc as _bacc
    from concourse import mybir as _mybir
    from concourse.bass_utils import run_bass_kernel_spmd as _run

    nc = _bacc.Bacc("TRN2", target_bir_lowering=False, num_devices=1)
    arrays, args = {}, []
    for name in _INS:
        a = _np.ascontiguousarray(inputs[name])
        arrays[f"in_{name}_dram"] = a
        args.append(nc.dram_tensor(f"in_{name}_dram", a.shape, _mybir.dt.from_np(a.dtype), kind="ExternalInput").ap())
    for i, (shape, dtype) in enumerate(_OUTS):
        dt = _mybir.dt.from_np(_np.dtype(dtype))
        args.append(nc.dram_tensor(f"out_{i}_dram", shape, dt, kind="ExternalOutput").ap())
    cond_resid_kernel(nc, *args)
    r = _run(nc, [arrays], core_ids=[0])
    got = tuple(r.results[0][f"out_{i}_dram"] for i in range(len(_OUTS)))
    return got[0]
```

```python
from collections import namedtuple
from contextlib import ExitStack

import concourse.bass as bass
from concourse import mybir

ALU = mybir.AluOpType
ACT = mybir.ActivationFunctionType
AX_X = mybir.AxisListType.X
F32 = mybir.dt.float32
BF16 = mybir.dt.bfloat16

P = 128
LAYERS = 3
NEG = -1e30
EPS = 1e-8
CLAMP = 256.0

LEFT_PARTS = "hhhmml"
RIGHT_PARTS = "lmhhmh"

Step = namedtuple("Step", "i par uses")


def following(s):
    return Step(s.i + 1, 1 - s.par, s.uses + s.par)


def preceding(s):
    return Step(s.i - 1, 1 - s.par, s.uses - (1 - s.par))


def wait(eng, sem, count):
    if isinstance(count, int) and count <= 0:
        return
    eng.wait_ge(sem, count)


def held(eng, *values):
    return [v if isinstance(v, int) else eng.snap(v) for v in values]


def cond_resid_kernel(nc, x, cond, ka_w, ka_b, k_w, k_b, oa_w, oa_b, o_w, o_b, w1, b1, la_w, la_b,
                      down, dgamma, dbeta, up, ugamma, ubeta, w_dec, b_dec, v_mat, out):
    B, N, F = x.shape
    S = cond.shape[1]
    H = 16
    D = F // H
    KC = F // P
    RANK = v_mat.shape[0]
    HID = down.shape[1]
    NB = 2
    T = NB * N
    STEPS = B // NB
    Q = T // P
    CH = 4
    XT = 8
    G = T // XT
    GC = G // CH
    GAIN = 1.0 / float(S) ** 0.5
    PLACED = len(LEFT_PARTS) + len(RIGHT_PARTS)
    NDEC = w_dec.shape[1]
    UCH = 16
    assert (B, N, F, S, D, KC, XT * H) == (16, 256, 256, P, 16, 2, P) and NDEC == (F + 1) * RANK

    x_rows = x.rearrange("b n f -> (b n) f")
    out_rows = out.rearrange("b n f -> (b n) f")
    rows_dram = nc.dram_tensor("rows_dram", (B, 2 * HID + 2 * F), F32, kind="Internal").ap()
    u_dram = nc.dram_tensor("u_dram", (B, UCH * 512), F32, kind="Internal").ap()
    keys_dram = nc.dram_tensor("keys_dram", (2, 4, H, 2, D, G), F32, kind="Internal").ap()

    with ExitStack() as ctx:
        def sb(name, shape, dt=F32):
            return ctx.enter_context(nc.sbuf_tensor(name, shape, dt))

        def sem(name):
            return ctx.enter_context(nc.semaphore(name))

        ident = sb("ident", [P, P])
        cond_t = sb("cond_t", [P, 32])
        table_a = sb("table_a", [P, STEPS, 8])
        table_c = sb("table_c", [P, STEPS, 17])
        cur_a = sb("cur_a", [P, 8])
        cur_c = sb("cur_c", [P, 2, 17])
        w_t = sb("w_t", [P, LAYERS, KC, F])
        down_sb = sb("down_sb", [P, KC, HID])
        up_pad = sb("up_pad", [P, NB, F])
        v_pad = sb("v_pad", [P, NB, F])
        u_all = sb("u_all", [P, B, KC, RANK])
        biases = sb("biases", [P, 9, KC])
        eps_t = sb("eps_t", [P, 96])
        b_dec_t = sb("b_dec_t", [P, KC, RANK])
        ybias = sb("ybias", [P, STEPS])
        b_dec_c = sb("b_dec_c", [P, 1])
        mask = sb("mask", [P, 2, T], BF16)
        style = sb("style", [P, 6, B])
        style2 = sb("style2", [P, 6, B])
        x_in = sb("x_in", [P, 2, Q, F])
        x_t = sb("x_t", [P, KC, T])
        x_res = sb("x_res", [P, 2, KC, T])
        keys = sb("keys", [P, KC, T])
        rest = sb("rest", [P, KC, T])
        part = {c: sb(f"part_{c}", [P, KC, T], BF16) for c in "hml"}
        gram = sb("gram", [P, 2, 2, H, T], BF16)
        keys_v = sb("keys_v", [P, 2, D, G])
        z = sb("z", [P, 2, GC, 32])
        z_t = sb("z_t", [P, 2, GC, 32])
        diag = sb("diag", [P, 2, GC, P])
        row_max = sb("row_max", [P, 2, GC])
        row_sum = sb("row_sum", [P, 2, GC])
        row_inv = sb("row_inv", [P, 2, GC])
        o_rows = sb("o_rows", [P, H, XT, GC])
        o_t = sb("o_t", [P, KC, CH, XT, GC])
        y = sb("y", [P, KC, T])
        x1 = sb("x1", [P, KC, T])
        x2 = sb("x2", [P, KC, T])
        x3 = sb("x3", [P, KC, T])
        act2 = sb("act2", [P, N])
        y3 = sb("y3", [P, N])
        out_sb = sb("out_sb", [P, Q, F])
        w_mod = [sb(f"w_mod{n}", [P, NB, KC, F]) for n in range(LAYERS)]
        down_row = sb("down_row", [P, NB, 2, HID])
        up_row = sb("up_row", [P, F])
        beta_pad = sb("beta_pad", [P, NB, F])
        w_down = sb("w_down", [P, NB, KC, HID])
        w_up_pad = sb("w_up_pad", [P, NB, F])
        u_pad = sb("u_pad", [P, NB, KC, HID])
        raw = diag[:, :, :, :].rearrange("p a g c -> p (a g c)")
        raw_w = raw[:, 0:1536].rearrange("p (l k f) -> p l k f", l=LAYERS, k=KC)
        w_sq = raw[:, 1536:3072].rearrange("p (l k f) -> p l k f", l=LAYERS, k=KC)
        raw_a = raw[:, 3072:3840].rearrange("p (l k s) -> p l k s", l=LAYERS, k=KC)
        raw_c = raw[:, 3840:3968]
        aff_t = z[:, :, :, :].rearrange("p a g c -> p (a g c)")[:, 0:768].rearrange("p (l f) -> p l f", l=LAYERS)
        gb = x3[:, :, :].rearrange("p k t -> p (k t)")
        gamma_beta = gb[:, 0:640]
        row_sb = z_t[:, :, :, :].rearrange("p a g c -> p (a g c)")[:, 0:640]
        o_w_perm = y[:, :, :].rearrange("p k t -> p (k t)")[:, 0:512].rearrange("p (o c i) -> p o c i", o=KC, c=KC)
        w_dec_sb = gram[:, 1].rearrange("p a h t -> p (a h t)").bitcast(F32)[:, 0:NDEC]
        u_sb = o_rows[:, :, :, :].rearrange("p h x g -> p (h x g)").rearrange("p (k n) -> p k n", n=512)

        psum = ctx.enter_context(nc.psum_tensor("psum", [P, 8, 512], F32))
        SC, OB, PA, PC = 0, 2, 4, 6
        pa = psum[:, PA:PA + 2, :]
        pc = psum[:, PC:PC + 2, :]

        def rest_banks(c):
            return pa if isinstance(c.i, int) and c.i == STEPS - 1 else pc

        ld_k = sem("ld_k")
        ld_w = sem("ld_w")
        ld_g = sem("ld_g")
        ld_wdec = sem("ld_wdec")
        ld_pads = sem("ld_pads")
        ld_bias_k = sem("ld_bias_k")
        ld_bias = sem("ld_bias")
        ld_x = [sem(f"ld_x{p}") for p in range(2)]
        st_rows = sem("st_rows")
        st_u = sem("st_u")
        ld_u = sem("ld_u")
        ld_gate = sem("ld_gate")
        st_keys = [sem(f"st_keys{p}") for p in range(2)]
        ld_keys = [sem(f"ld_keys{p}") for p in range(2)]
        ld_gram = [sem(f"ld_gram{p}") for p in range(2)]
        ld_o = sem("ld_o")
        st_out = sem("st_out")
        ident_0 = sem("ident_0")
        ident_1 = sem("ident_1")
        pads_done = sem("pads_done")
        mask_base = sem("mask_base")
        mask_done = sem("mask_done")
        ld_mask = [sem(f"ld_mask{p}") for p in range(2)]
        diag_zero = sem("diag_zero")
        su_perm = sem("su_perm")
        su_t = sem("su_t")
        su_aff = sem("su_aff")
        su_ev = sem("su_ev")
        su_sq = sem("su_sq")
        su_style = sem("su_style")
        su_rows = sem("su_rows")
        su_rows_ev = sem("su_rows_ev")
        su_st = sem("su_st")
        su_dem = sem("su_dem")
        su_var = sem("su_var")
        su_sqrt = sem("su_sqrt")
        su_tab = sem("su_tab")
        su_u = sem("su_u")
        su_u_ev = sem("su_u_ev")
        su_o0 = sem("su_o0")
        su_uadd = sem("su_uadd")
        cur_a_set = sem("cur_a_set")
        wk_done = sem("wk_done")
        xt_mm = sem("xt_mm")
        xt_ev = sem("xt_ev")
        k_mm = sem("k_mm")
        keys_ev = sem("keys_ev")
        res_done = sem("res_done")
        h_done = sem("h_done")
        r1_done = sem("r1_done")
        m_done = sem("m_done")
        l_done = sem("l_done")
        g_mm = sem("g_mm")
        max_done = sem("max_done")
        z_done = sem("z_done")
        exp_done = sem("exp_done")
        sum_done = sem("sum_done")
        inv_done = sem("inv_done")
        norm_done = sem("norm_done")
        zt_done = sem("zt_done")
        diag_done = sem("diag_done")
        av_mm = sem("av_mm")
        o_ev = sem("o_ev")
        cur_c_set = sem("cur_c_set")
        wo_done = sem("wo_done")
        w1_done = sem("w1_done")
        gate_mul_p = sem("gate_mul_p")
        gate_mul = sem("gate_mul")
        u_done = sem("u_done")
        c1_mm = sem("c1_mm")
        x1_done = sem("x1_done")
        c2_mm = sem("c2_mm")
        c2_ev = sem("c2_ev")
        clip_done = sem("clip_done")
        x2_done = sem("x2_done")
        c3_mm = sem("c3_mm")
        act_done = sem("act_done")
        c4_mm = sem("c4_mm")
        x3_done = sem("x3_done")
        c5_mm = sem("c5_mm")
        y3_done = sem("y3_done")
        c6_mm = sem("c6_mm")
        x4_done = sem("x4_done")
        c7_mm = sem("c7_mm")
        out_ev = sem("out_ev")

        W_BANK = (2, 3, 2)
        SUM_BANK = (7, 1)
        DEM = (slice(0, 2 * B), slice(2 * B, 6 * B))

        block = ctx.enter_context(nc.Block())

        def perm(ap):
            return ap.rearrange("p (a c d) -> p c d a", a=H // 2, c=KC)

        def steps(eng, body):
            body(Step(0, 0, 0), "XPSB")
            body(Step(1, 1, 0), "XKPSBC")
            with eng.Fori(0, (STEPS - 4) // 2) as m:
                body(Step(2 * m + 2, 0, m + 1), "XKPSBC")
                body(Step(2 * m + 3, 1, m + 1), "XKPSBC")
            body(Step(STEPS - 2, 0, STEPS // 2 - 1), "KPSBC")
            body(Step(STEPS - 1, 1, STEPS // 2 - 1), "BC")
            body(Step(STEPS, 0, STEPS // 2), "C")

        @block.sync
        def _(sp):
            def load(dst, src, s):
                sp.dma_start(dst, src).then_inc(s, 16)

            def load_biases(which, s):
                with nc.allow_non_contiguous_dma(reason="bias columns"):
                    for n, v, permuted in which:
                        order = "(a c d) -> d a c" if permuted else "(c p) -> p c"
                        sizes = {"a": H // 2, "c": KC} if permuted else {"c": KC}
                        load(biases[:, n, :], v.rearrange(order, **sizes), s)

            def decoder_out():
                sp.wait_ge(su_u_ev, 4)
                for c in range(4):
                    dst = u_dram.rearrange("b (k c n) -> c b k n", c=4, n=512)[c]
                    if c < 3:
                        sp.dma_start(dst, u_sb[32 * c:32 * c + B, :, :]).then_inc(st_u, 16)
                    else:
                        sp.dma_start(dst[:, 0:3, :], u_sb[96:96 + B, 0:3, :]).then_inc(st_u, 16)
                        last = NDEC - (UCH - 1) * 512
                        sp.dma_start(dst[:, 3, 0:last], u_sb[96:96 + B, 3, 0:last]).then_inc(st_u, 16)

            def decoder_in():
                sp.wait_ge(st_u, 16 * 5)
                with nc.allow_non_contiguous_dma(reason="bias columns"):
                    for c in range(KC):
                        src = u_dram[:, c * P * RANK:(c + 1) * P * RANK].rearrange("b (p k) -> p b k", k=RANK)
                        sp.dma_start(u_all[:, :, c, :], src).then_inc(ld_u, 16)
                    for b in range(NB):
                        src = u_dram.rearrange("(s b) n -> b n s", b=NB)[b][F * RANK:(F + 1) * RANK, :]
                        sp.dma_start(ybias[64 * b:64 * b + RANK, :], src).then_inc(ld_u, 16)

            def gates(s):
                used, first = held(sp, 2 * s.i, NB * s.i)
                rows = rows_dram[bass.ds(first, NB), :]
                wait(sp, gate_mul, used)
                sp.dma_start(down_row[:, :, :, :].rearrange("p b a h -> p b (a h)"),
                             rows[:, 0:2 * HID].unsqueeze(0).to_broadcast([P, NB, 2 * HID])).then_inc(ld_gate, 16)
                gamma, beta = rows[:, 2 * HID:2 * HID + F], rows[:, 2 * HID + F:2 * HID + 2 * F]
                sp.dma_start(up_row[:, :], gamma.unsqueeze(1).to_broadcast([NB, HID, F])).then_inc(ld_gate, 16)
                for b in range(NB):
                    sp.dma_start(beta_pad[HID * b:HID * (b + 1), b, :], beta[b:b + 1, :].to_broadcast([HID, F]))\
                        .then_inc(ld_gate, 16)

            def mask_rows(par):
                for side in range(2):
                    sp.dma_start(gram[96:98, par, side],
                                 mask[96:98, side, :].unsqueeze(1).to_broadcast([2, H, T]))\
                        .then_inc(ld_mask[par], 16)

            def spread(a):
                evacuated, read, split, stored = held(sp, 4 * (a.i + 1), CH * (a.i - 1), a.i + 1, 64 * (a.uses + 1))
                sp.wait_ge(keys_ev, evacuated)

                def store_keys(q):
                    sp.dma_start(keys_dram[a.par, q].rearrange("j t d g -> d (j t) g"),
                                 keys[:, :, :].rearrange("p b (t q g) -> p (b t) q g", t=2, q=4)[:, :, q, :])\
                        .then_inc(st_keys[a.par], 16)

                start = isinstance(a.i, int) and a.i == 0
                if not start:
                    store_keys(0)
                    store_keys(1)
                wait(sp, g_mm, read)
                if isinstance(a.i, int) and a.i == 1:
                    sp.wait_ge(su_u, UCH)
                    mask_rows(1)
                for c, done in (("h", h_done), ("m", m_done), ("l", l_done)):
                    sp.wait_ge(done, split)
                    for side, order in enumerate((LEFT_PARTS, RIGHT_PARTS)):
                        for g, o in enumerate(order):
                            if o == c:
                                sp.dma_start(gram[16 * g:16 * g + 16, a.par, side, :, :], part[c][:, :, :])\
                                    .then_inc(ld_gram[a.par], 16)
                    if c == "m" and not start:
                        store_keys(2)
                        store_keys(3)
                if start:
                    for q in range(4):
                        store_keys(q)
                    sp.wait_ge(su_rows_ev, 2)
                    sp.dma_start(rows_dram, row_sb[0:B, :]).then_inc(st_rows, 16)
                sp.wait_ge(st_keys[a.par], stored)
                wait(sp, av_mm, read)
                sp.dma_start(keys_v[:, a.par, :, :], keys_dram[a.par].rearrange("q j t d g -> (q j t) d g"))\
                    .then_inc(ld_keys[a.par], 16)

            def load_x(a):
                first, used = held(sp, a.i * T, 2 * (a.i - 1))
                rows = x_rows[bass.ds(first, T), :].rearrange("(q p) f -> p q f", p=P)
                wait(sp, xt_mm, used)
                sp.dma_start(x_in[:, a.par], rows).then_inc(ld_x[a.par], 16)

            def body(s, stages):
                if "X" in stages:
                    load_x(following(following(s)))
                if "P" in stages:
                    spread(following(s))
                if isinstance(s.i, int) and s.i == 0:
                    decoder_in()
                if "B" in stages:
                    sp.wait_ge(o_ev, CH * (s.i + 1))
                    for t in range(CH):
                        sp.dma_start(o_t[:, :, t].rearrange("p k x g -> p k (x g)"),
                                     o_rows[32 * t:32 * t + D].rearrange("p h x g -> p h (x g)")).then_inc(ld_o, 16)
                    gates(s)
                if "C" in stages:
                    c = preceding(s)
                    first, ready = held(sp, c.i * T, 2 * (c.i + 1))
                    rows = out_rows[bass.ds(first, T), :].rearrange("(q p) f -> p q f", p=P)
                    sp.wait_ge(out_ev, ready)
                    sp.dma_start(rows, out_sb[:, :, :]).then_inc(st_out, 16)

            load(raw_c[0:B, :], cond, ld_k)
            load(raw_a[:, 0], ka_w.rearrange("(k p) s -> p k s", p=P), ld_k)
            for c in range(KC):
                load(raw_w[:, 0, c], k_w.rearrange("(a c d) i -> c d a i", a=H // 2, c=KC)[c], ld_k)
            load(x_in[:, 0], x_rows[0:T, :].rearrange("(q p) f -> p q f", p=P), ld_x[0])
            load_biases(((0, ka_b, False), (3, k_b, True)), ld_bias_k)
            load(w_dec_sb, w_dec, ld_wdec)
            for n, w in ((1, oa_w), (2, la_w)):
                load(raw_a[:, n], w.rearrange("(k p) s -> p k s", p=P), ld_w)
            for n, w in ((1, o_w), (2, w1)):
                load(raw_w[:, n], w.rearrange("(k p) i -> p k i", p=P), ld_w)
            load_biases(((4, o_b, False), (1, oa_b, True), (2, la_b, False), (5, b1, False)), ld_bias)
            load_x(Step(1, 1, 0))
            for w, o in ((dgamma, 0), (dbeta, HID), (ugamma, 2 * HID), (ubeta, 2 * HID + F)):
                load(gamma_beta[:, o:o + w.shape[1]], w, ld_g)
            load(down_sb[:, :, :], down.rearrange("(k p) h -> p k h", p=P), ld_g)
            sp.wait_ge(mask_done, 2)
            mask_rows(0)
            spread(Step(0, 0, 0))
            decoder_out()
            sp.wait_ge(st_rows, 16)
            steps(sp, body)
            sp.wait_ge(st_out, 16 * STEPS)

        @block.gpsimd
        def _(pool):
            pool.memset(ident[:, :], 0.0).then_inc(ident_0, 1)
            pool.wait_ge(ident_0, 1)
            pool.affine_select(out=ident[:, :], in_=ident[:, :], compare_op=ALU.not_equal, fill=1.0,
                               base=0, pattern=[[-1, P]], channel_multiplier=1).then_inc(ident_1, 1)
            pool.memset(cond_t[:, :], 0.0).then_inc(pads_done, 1)
            pool.memset(v_pad[:, :, :], 0.0).then_inc(pads_done, 1)
            pool.memset(b_dec_c[:, :], 0.0).then_inc(pads_done, 1)
            pool.memset(ybias[:, :], 0.0).then_inc(pads_done, 1)
            pool.memset(u_pad[:, :, :, :], 0.0).then_inc(pads_done, 1)
            pool.memset(beta_pad[:, :, :], 0.0).then_inc(pads_done, 1)
            pool.memset(up_pad[:, :, :], 0.0).then_inc(pads_done, 1)

            left, right = (mask[96:98, side, :].rearrange("p (t g) -> p t g", t=2) for side in range(2))
            pool.wait_ge(pads_done, 7)
            pool.memset(left, 1.0).then_inc(mask_base, 1)
            pool.memset(right, 0.0).then_inc(mask_base, 1)
            pool.wait_ge(mask_base, 2)
            for ap, fill in ((left, 0.0), (right, NEG)):
                pool.affine_select(out=ap, in_=ap, compare_op=ALU.is_equal, fill=fill, base=0,
                                   pattern=[[-1, 2], [0, N]], channel_multiplier=1).then_inc(mask_done, 1)
            with nc.allow_non_contiguous_dma(reason="bias columns"):
                pool.wait_ge(pads_done, 7)
                for b in range(NB):
                    pool.dma_start(up_pad[HID * b:HID * (b + 1), b, :], up).then_inc(ld_pads, 16)
                    pool.dma_start(v_pad[64 * b:64 * b + RANK, b, :], v_mat).then_inc(ld_pads, 16)
                    pool.dma_start(b_dec_c[64 * b:64 * b + RANK, :],
                                   b_dec[F * RANK:(F + 1) * RANK].rearrange("(k o) -> k o", o=1))\
                        .then_inc(ld_pads, 16)
                for c in range(KC):
                    pool.dma_start(b_dec_t[:, c, :], b_dec[c * P * RANK:(c + 1) * P * RANK]
                                   .rearrange("(p k) -> p k", k=RANK)).then_inc(ld_pads, 16)
            def normalise(s, n):
                pool.wait_ge(inv_done, CH * s.i + n + 1)
                pool.wait_ge(exp_done, CH * s.i + n + 1)
                b = n % 2
                pool.tensor_tensor(z[:, b], z[:, b], row_inv[:, b, :].unsqueeze(2).to_broadcast([P, GC, 32]),
                                   ALU.mult).then_inc(norm_done, 1)

            def residue(a):
                pool.wait_ge(h_done, a.i + 1)
                wait(pool, l_done, a.i)
                pool.tensor_tensor(rest[:, :, :], keys[:, :, :], part["h"][:, :, :], ALU.subtract)\
                    .then_inc(r1_done, 1)

            def modulate(n, c, col, done):
                styles = cur_c[:, c.par, col:col + 4].rearrange("p (k b) -> p b k", b=NB)
                pool.tensor_tensor(w_mod[n][:, :, :, :], w_t[:, n].unsqueeze(1).to_broadcast([P, NB, KC, F]),
                                   styles.unsqueeze(3).to_broadcast([P, NB, KC, F]), ALU.mult).then_inc(done, 1)

            def modulate_low_rank(c):
                pool.wait_ge(ld_gate, 64 * (c.i + 1))
                wait(pool, c4_mm, 2 * c.i)
                for b in range(NB):
                    gam = down_row[:, b, 0, :].unsqueeze(1).to_broadcast([P, KC, HID])
                    pool.tensor_tensor(w_down[:, b], down_sb[:, :, :], gam, ALU.mult).then_inc(gate_mul_p, 1)
                pool.tensor_tensor(w_up_pad[:, :, :], up_pad[:, :, :],
                                   up_row[:, :].unsqueeze(1).to_broadcast([P, NB, F]), ALU.mult)\
                    .then_inc(gate_mul_p, 1)
                pool.wait_ge(gate_mul_p, 3 * (c.i + 1))
                for b in range(NB):
                    beta = down_row[:, b, 1, :].unsqueeze(1).to_broadcast([P, KC, HID])
                    mul = pool.tensor_tensor(w_down[:, b], w_down[:, b], beta, ALU.add)
                mul.then_inc(gate_mul, 1)
                pool.tensor_tensor(w_up_pad[:, :, :], w_up_pad[:, :, :], beta_pad[:, :, :], ALU.add)\
                    .then_inc(gate_mul, 1)

            def body(s, stages):
                c = preceding(s)
                if "B" in stages:
                    normalise(s, 0)
                    normalise(s, 1)
                if "P" in stages:
                    residue(following(s))
                if "C" in stages:
                    modulate_low_rank(c)
                if "B" in stages:
                    normalise(s, 2)
                    normalise(s, 3)
                if "B" in stages:
                    pool.wait_ge(cur_c_set, s.i + 1)
                    wait(pool, c1_mm, 2 * s.i)
                    modulate(1, s, 0, wo_done)
                    wait(pool, c2_mm, 2 * s.i)
                    modulate(2, s, 8, w1_done)
                if isinstance(s.i, int) and s.i == 0:
                    pool.wait_ge(ld_u, 64)
                    pool.wait_ge(ld_pads, 16 * 8)
                    pool.tensor_tensor(table_c[:, :, 16], ybias[:, :], b_dec_c[:, :].to_broadcast([P, STEPS]),
                                       ALU.add).then_inc(su_uadd, 1)
                    pool.tensor_tensor(u_all[:, :, :, :], u_all[:, :, :, :],
                                       b_dec_t[:, :, :].rearrange("p c k -> p (c k)").unsqueeze(1)
                                       .to_broadcast([P, B, KC * RANK]).rearrange("p b (c k) -> p b c k", c=KC),
                                       ALU.add).then_inc(su_uadd, 1)

            pool.wait_ge(mask_done, 2)
            residue(Step(0, 0, 0))
            pool.wait_ge(su_dem, 2)
            pool.memset(diag[:, :, :, :], 0.0).then_inc(diag_zero, 1)
            steps(pool, body)

        @block.scalar
        def _(act):
            def weights(n):
                act.wait_ge(su_t, (2, 4, 5)[n])
                src = psum[:, W_BANK[n], :]
                act.activation(w_t[:, n].rearrange("p k f -> p (k f)"), src, ACT.Copy).then_inc(su_ev, 1)
                act.activation(w_sq[:, n].rearrange("p k f -> p (k f)"), src, ACT.Square).then_inc(su_sq, 1)

            def square_roots(n):
                act.wait_ge(su_var, n + 1)
                t = DEM[n]
                act.activation(eps_t[:, t], eps_t[:, t], ACT.Sqrt).then_inc(su_sqrt, 1)

            def x_evacuate(a):
                act.wait_ge(xt_mm, 2 * (a.i + 1))
                wait(act, k_mm, 2 * a.i)
                wait(act, res_done, 2 * a.i)
                act.activation(x_t[:, :, :], pa, ACT.Copy).then_inc(xt_ev, 1)

            def keys_evacuate(a):
                if isinstance(a.i, int) and a.i == 0:
                    act.wait_ge(ld_bias_k, 16 * 2)
                else:
                    before = preceding(a)
                    act.wait_ge(st_keys[before.par], 64 * (before.uses + 1))
                    act.wait_ge(r1_done, a.i)
                    act.wait_ge(h_done, a.i)
                act.wait_ge(cur_a_set, a.i + 1)
                for c in range(KC):
                    act.wait_ge(k_mm, 2 * a.i + c + 1)
                    for b in range(NB):
                        t = slice(N * b, N * (b + 1))
                        act.activation(keys[:, c, t], pa[:, c, t], ACT.Identity, bias=biases[:, 3, c:c + 1],
                                       scale=cur_a[:, 4 + 2 * c + b:5 + 2 * c + b]).then_inc(keys_ev, 1)

            def exponent(s, n):
                act.wait_ge(z_done, CH * s.i + n + 1)
                b = n % 2
                act.activation(z[:, b], z[:, b], ACT.Exp, scale=D ** -0.5).then_inc(exp_done, 1)

            def spread_diagonal(s, n):
                act.wait_ge(zt_done, CH * s.i + n + 1)
                wait(act, av_mm, CH * s.i + n - 1)
                if isinstance(s.i, int) and s.i == 0 and n == 0:
                    act.wait_ge(diag_zero, 1)
                b = n % 2
                for q in range(4):
                    r = slice(32 * q, 32 * q + 32)
                    act.activation(diag[r, b, :, r], z_t[r, b], ACT.Copy).then_inc(diag_done, 1)

            def evacuate_l1(c, o):
                act.wait_ge(c2_mm, 2 * c.i + o + 1)
                for b in range(NB):
                    t = slice(N * b, N * (b + 1))
                    k = 12 + 2 * o + b
                    act.activation(y[:, o, t], rest_banks(c)[:, o, t], ACT.Identity, bias=biases[:, 5, o:o + 1],
                                   scale=cur_c[:, c.par, k:k + 1]).then_inc(c2_ev, 1)

            def body(s, stages):
                c = preceding(s)
                ends = isinstance(s.i, int) and s.i == STEPS - 1
                if "B" in stages:
                    exponent(s, 1)
                if "K" in stages:
                    keys_evacuate(following(s))
                if "B" in stages:
                    spread_diagonal(s, 0)
                    spread_diagonal(s, 1)
                    exponent(s, 2)
                if ends:
                    exponent(s, 3)
                if "C" in stages:
                    act.wait_ge(cur_c_set, c.i + 1)
                    wait(act, x2_done, 2 * c.i)
                    evacuate_l1(c, 0)
                if ends:
                    spread_diagonal(s, 2)
                if "B" in stages and not ends:
                    exponent(s, 3)
                if "C" in stages:
                    evacuate_l1(c, 1)
                if "B" in stages:
                    spread_diagonal(s, 3 if ends else 2)
                if "C" in stages:
                    act.wait_ge(c3_mm, c.i + 1)
                    wait(act, c4_mm, 2 * c.i)
                    act.activation(act2[:, :], rest_banks(c)[:, 0, 0:N], ACT.Relu).then_inc(act_done, 1)
                if "B" in stages and not ends:
                    spread_diagonal(s, 3)
                if "X" in stages:
                    x_evacuate(following(following(s)))
                if "C" in stages:
                    act.wait_ge(c5_mm, c.i + 1)
                    wait(act, c6_mm, 2 * c.i)
                    act.activation(y3[:, :], rest_banks(c)[:, 0, 0:N], ACT.Identity, bias=cur_c[:, c.par, 16:17])\
                        .then_inc(y3_done, 1)
                if "S" in stages:
                    exponent(following(s), 0)
                if "C" in stages:
                    wait(act, st_out, 16 * c.i)
                    for o in range(2):
                        act.wait_ge(c7_mm, 2 * c.i + o + 1)
                        act.activation(out_sb[:, 2 * o:2 * o + 2, :].rearrange("p q f -> p (q f)"), rest_banks(c)[:, o, :],
                                       ACT.Copy).then_inc(out_ev, 1)

            weights(0)
            x_evacuate(Step(0, 0, 0))
            square_roots(0)
            keys_evacuate(Step(0, 0, 0))
            x_evacuate(Step(1, 1, 0))
            weights(1)
            weights(2)
            act.wait_ge(su_rows, 1)
            act.activation(row_sb[0:32, 0:2 * HID], psum[0:32, 3, 0:2 * HID], ACT.Copy).then_inc(su_rows_ev, 1)
            act.activation(row_sb[0:32, 2 * HID:640], psum[0:32, 0, :], ACT.Copy).then_inc(su_rows_ev, 1)
            square_roots(1)
            exponent(Step(0, 0, 0), 0)
            keys_evacuate(Step(1, 1, 0))
            steps(act, body)

        @block.vector
        def _(dve):
            def by_step(ap):
                return ap.rearrange("p c (s b) -> p c s b", b=NB)

            def columns(table, at):
                return table[:, :, at:at + 4].rearrange("p s (c b) -> p c s b", b=NB)

            def styles(n, layers):
                k = slice(2 * layers.start, 2 * layers.stop)
                dve.wait_ge(su_style, n + 1)
                cols = psum[:, SUM_BANK[n], k.start * B:k.stop * B].rearrange("p (k b) -> p k b", b=B)
                dve.tensor_tensor(style[:, k, :], cols, biases[:, layers, :].rearrange("p l c -> p (l c)")
                                  .unsqueeze(2).to_broadcast([P, k.stop - k.start, B]), ALU.add).then_inc(su_st, 1)
                dve.wait_ge(su_st, 3 * n + 1)
                dve.tensor_tensor(style2[:, k, :], style[:, k, :], style[:, k, :], ALU.mult).then_inc(su_st, 1)

            def demodulations(n):
                t = DEM[n]
                dve.wait_ge(su_dem, n + 1)
                dve.tensor_scalar(eps_t[:, t], psum[:, SUM_BANK[n], 96 + t.start:96 + t.stop], EPS, None, ALU.add)\
                    .then_inc(su_var, 1)
                dve.wait_ge(su_sqrt, n + 1)
                dem = style2[:, :, :].rearrange("p k b -> p (k b)")
                dve.reciprocal(dem[:, t], eps_t[:, t]).then_inc(su_st, 1)
                dve.wait_ge(su_st, 3 * n + 3)

            def prepare_a(a):
                wait(dve, keys_ev, 4 * a.i)
                dve.tensor_copy(cur_a[:, :], table_a[:, a.i, :]).then_inc(cur_a_set, 1)
                dve.wait_ge(cur_a_set, a.i + 1)
                wait(dve, k_mm, 2 * a.i)
                for b in range(NB):
                    for c in range(KC):
                        dve.tensor_scalar(w_mod[0][:, b, c, :], w_t[:, 0, c, :],
                                          cur_a[:, 2 * c + b:2 * c + b + 1], None, ALU.mult).then_inc(wk_done, 1)

            def keep_x(a):
                dve.wait_ge(xt_ev, a.i + 1)
                for c in range(KC):
                    dve.tensor_scalar(x_res[:, a.par, c, :], x_t[:, c, :], biases[:, 4, c:c + 1], None, ALU.add)\
                        .then_inc(res_done, 1)

            def split_high(a):
                dve.wait_ge(keys_ev, 4 * (a.i + 1))
                if not (isinstance(a.i, int) and a.i == 0):
                    before = preceding(a)
                    dve.wait_ge(ld_gram[before.par], 16 * PLACED * (before.uses + 1))
                dve.tensor_copy(part["h"][:, :, :], keys[:, :, :]).then_inc(h_done, 1)

            def split_middle(a):
                dve.wait_ge(r1_done, a.i + 1)
                dve.tensor_copy(part["m"][:, :, :], rest[:, :, :]).then_inc(m_done, 1)

            def split_low(a):
                dve.wait_ge(m_done, a.i + 1)
                dve.tensor_tensor(part["l"][:, :, :], rest[:, :, :], part["m"][:, :, :], ALU.subtract)\
                    .then_inc(l_done, 1)

            def shift(s, n):
                k = CH * s.i + n
                b = n % 2
                dve.wait_ge(g_mm, k + 1)
                scores = psum[:, SC + b, :].rearrange("p (g j) -> p g j", j=32)
                dve.tensor_reduce(row_max[:, b, :], scores, AX_X, ALU.max).then_inc(max_done, 1)
                dve.wait_ge(max_done, k + 1)
                wait(dve, zt_done, k - 1)
                dve.tensor_tensor(z[:, b], scores, row_max[:, b, :].unsqueeze(2).to_broadcast([P, GC, 32]),
                                  ALU.subtract).then_inc(z_done, 1)

            def row_sums(s, n):
                k = CH * s.i + n
                b = n % 2
                dve.wait_ge(exp_done, k + 1)
                dve.tensor_reduce(row_sum[:, b, :], z[:, b], AX_X, ALU.add).then_inc(sum_done, 1)
                dve.wait_ge(sum_done, k + 1)
                wait(dve, norm_done, k - 1)
                dve.reciprocal(row_inv[:, b, :], row_sum[:, b, :]).then_inc(inv_done, 1)

            def transpose(s, n):
                k = CH * s.i + n
                b = n % 2
                dve.wait_ge(norm_done, k + 1)
                wait(dve, diag_done, 4 * (k - 1))
                dve.transpose(z_t[:, b].rearrange("p g j -> p (g j)"), z[:, b].rearrange("p g j -> p (g j)"))\
                    .then_inc(zt_done, 1)

            def o_evacuate(s, n):
                k = CH * s.i + n
                dve.wait_ge(av_mm, k + 1)
                if n == 0:
                    wait(dve, ld_o, 64 * s.i)
                    if isinstance(s.i, int) and s.i == 0:
                        dve.wait_ge(st_u, 16 * 5)
                src = psum[:, OB + n % 2, :].rearrange("p (r q h) -> p r q h", r=4, q=4)
                dst = o_rows[:, :, :, n * 4:n * 4 + 4].rearrange("p h (t q) r -> p r q (h t)", t=2)
                dve.tensor_copy(dst, src).then_inc(o_ev, 1)

            def add_l0(c, o):
                dve.wait_ge(c1_mm, 2 * c.i + o + 1)
                for b in range(NB):
                    t = slice(N * b, N * (b + 1))
                    k = 4 + 2 * o + b
                    last = dve.scalar_tensor_tensor(x1[:, o, t], rest_banks(c)[:, o, t], cur_c[:, c.par, k:k + 1],
                                                    x_res[:, c.par, o, t], ALU.mult, ALU.add)
                last.then_inc(x1_done, 1)

            def add_l1(c, o):
                dve.wait_ge(c2_ev, 4 * c.i + 2 * o + 2)
                dve.tensor_scalar(y[:, o, :], y[:, o, :], -CLAMP, CLAMP, ALU.max, ALU.min).then_inc(clip_done, 1)
                dve.wait_ge(clip_done, 2 * c.i + o + 1)
                dve.tensor_tensor(x2[:, o, :], y[:, o, :], x1[:, o, :], ALU.add).then_inc(x2_done, 1)

            def take_columns(s):
                wait(dve, y3_done, s.i - 1)
                dve.tensor_copy(cur_c[:, s.par, 0:16], table_c[:, s.i, 0:16]).then_inc(cur_c_set, 1)

            def body(s, stages):
                c = preceding(s)
                a = following(s)
                ends = isinstance(s.i, int) and s.i == STEPS - 1
                if "B" in stages:
                    transpose(s, 0)
                    row_sums(s, 1)
                if "K" in stages:
                    split_high(a)
                if "C" in stages:
                    dve.wait_ge(cur_c_set, c.i + 1)
                    dve.wait_ge(res_done, 2 * (c.i + 1))
                    wait(dve, x2_done, 2 * c.i)
                    add_l0(c, 0)
                if "B" in stages:
                    transpose(s, 1)
                if "C" in stages:
                    add_l0(c, 1)
                if "P" in stages:
                    split_middle(a)
                if "B" in stages:
                    shift(s, 2)
                    shift(s, 3)
                    row_sums(s, 2)
                if ends:
                    row_sums(s, 3)
                    transpose(s, 2)
                    o_evacuate(s, 0)
                    transpose(s, 3)
                    o_evacuate(s, 1)
                if "C" in stages:
                    add_l1(c, 0)
                if "B" in stages and not ends:
                    row_sums(s, 3)
                    transpose(s, 2)
                if "C" in stages:
                    add_l1(c, 1)
                if "B" in stages and not ends:
                    o_evacuate(s, 0)
                    transpose(s, 3)
                if "P" in stages:
                    split_low(a)
                if "B" in stages and not ends:
                    o_evacuate(s, 1)
                    o_evacuate(s, 2)
                if ends:
                    take_columns(s)
                    o_evacuate(s, 2)
                    o_evacuate(s, 3)
                if "C" in stages:
                    wait(dve, c7_mm, 2 * c.i)
                    for o in range(KC):
                        dve.wait_ge(c4_mm, 2 * c.i + o + 1)
                        dve.scalar_tensor_tensor(x3[:, o, :], x2[:, o, :], 2.0, rest_banks(c)[:, o, :], ALU.mult, ALU.add)\
                            .then_inc(x3_done, 1)
                if "B" in stages and not ends:
                    take_columns(s)
                if "P" in stages:
                    keep_x(a)
                if "X" in stages:
                    prepare_a(following(a))
                if "B" in stages and not ends:
                    o_evacuate(s, 3)
                if "S" in stages:
                    shift(a, 0)
                if "C" in stages:
                    for o in range(KC):
                        dve.wait_ge(c6_mm, 2 * c.i + o + 1)
                        dve.tensor_tensor(x3[:, o, :], rest_banks(c)[:, o, :], x3[:, o, :], ALU.add).then_inc(x4_done, 1)
                if "S" in stages:
                    row_sums(a, 0)
                    shift(a, 1)
                if "B" in stages:
                    if isinstance(s.i, int) and s.i == 0:
                        dve.wait_ge(su_uadd, 2)
                    wait(dve, c5_mm, s.i)
                    dve.tensor_copy(cur_c[:, s.par, 16:17], table_c[:, s.i, 16:17]).then_inc(u_done, 1)
                    dve.tensor_copy(u_pad[:, :, :, 0:RANK], u_all[:, bass.ds(NB * s.i, NB), :, :])\
                        .then_inc(u_done, 1)

            dve.wait_ge(su_t, 1)
            dve.wait_ge(pads_done, 7)
            dve.tensor_copy(aff_t[:, 0, :], psum[:, 0, 0:F]).then_inc(su_aff, 1)
            dve.tensor_copy(cond_t[:, 0:B], psum[:, 1, F:F + B]).then_inc(su_aff, 1)
            dve.wait_ge(ld_bias_k, 16 * 2)
            styles(0, slice(0, 1))
            dve.tensor_copy(columns(table_a, 0), by_step(style[:, 0:2, :])).then_inc(su_tab, 1)
            dve.wait_ge(su_ev, 1)
            dve.wait_ge(su_tab, 1)
            for b in range(NB):
                for c in range(KC):
                    dve.tensor_scalar(w_mod[0][:, b, c, :], w_t[:, 0, c, :],
                                      table_a[:, 0, 2 * c + b:2 * c + b + 1], None, ALU.mult).then_inc(wk_done, 1)
            demodulations(0)
            dve.tensor_copy(columns(table_a, 4), by_step(style2[:, 0:2, :])).then_inc(su_tab, 1)
            dve.wait_ge(su_tab, 2)
            dve.tensor_copy(cur_a[:, :], table_a[:, 0, :]).then_inc(cur_a_set, 1)
            first = Step(0, 0, 0)
            split_high(first)
            dve.wait_ge(ld_w, 16 * 4)
            for o in range(KC):
                dve.tensor_copy(o_w_perm[:, o].rearrange("p c (d a) -> p c d a", d=D), perm(raw_w[:, 1, o, :]))\
                    .then_inc(su_perm, 1)
            dve.wait_ge(ld_bias, 16 * 4)
            keep_x(first)
            dve.wait_ge(su_u, UCH // 2)
            dve.tensor_copy(u_sb[:, 0:2, :], psum[:, 6:8, :]).then_inc(su_u_ev, 1)
            dve.wait_ge(su_t, 3)
            dve.tensor_copy(aff_t[:, 1, :].rearrange("p (c d a) -> p c d a", c=KC, d=D), perm(psum[:, 0, F:2 * F]))\
                .then_inc(su_aff, 1)
            dve.tensor_scalar(aff_t[:, 2, :], psum[:, 1, 0:F], GAIN, None, ALU.mult).then_inc(su_aff, 1)
            split_middle(first)
            split_low(first)
            prepare_a(following(first))
            styles(1, slice(1, 3))
            dve.tensor_copy(columns(table_c, 0), by_step(style[:, 2:4, :])).then_inc(su_tab, 1)
            dve.tensor_copy(columns(table_c, 8), by_step(style[:, 4:6, :])).then_inc(su_tab, 1)
            demodulations(1)
            dve.tensor_copy(columns(table_c, 4), by_step(style2[:, 2:4, :])).then_inc(su_tab, 1)
            dve.tensor_copy(columns(table_c, 12), by_step(style2[:, 4:6, :])).then_inc(su_tab, 1)
            dve.wait_ge(su_ev, 3)
            dve.wait_ge(su_sq, 3)
            dve.wait_ge(su_rows_ev, 1)
            dve.memset(psum[:, OB:OB + 2, :], 0.0).then_inc(su_o0, 1)
            dve.wait_ge(su_u, UCH)
            dve.tensor_copy(u_sb[:, 2, :], psum[:, 6, :]).then_inc(su_u_ev, 1)
            dve.tensor_copy(u_sb[0:96, 3, :], psum[0:96, 7, :]).then_inc(su_u_ev, 1)
            last = NDEC - (UCH - 1) * 512
            dve.tensor_copy(u_sb[96:128, 3, 0:last], psum[96:128, 7, 0:last]).then_inc(su_u_ev, 1)
            shift(first, 0)
            shift(first, 1)
            row_sums(first, 0)
            split_high(following(first))
            dve.wait_ge(st_rows, 16)
            steps(dve, body)

        @block.tensor
        def _(pe):
            mm = nc.tensor.matmul
            def affine_transposes(n):
                for c in range(KC):
                    k = 2 * n + c
                    last = nc.tensor.transpose(psum[:, k // 4, (k % 4) * P:(k % 4 + 1) * P], raw_a[:, n, c, :],
                                               ident[:, :])
                return last

            def weight_transposes(n):
                for c in range(KC):
                    for o in range(KC):
                        src = raw_w[:, n, o, :]
                        src = o_w_perm[:, o, c, :] if n == 1 else src[:, c * P:(c + 1) * P]
                        k = 2 * c + o
                        last = nc.tensor.transpose(psum[:, W_BANK[n], k * P:(k + 1) * P], src, ident[:, :])
                last.then_inc(su_t, 1)

            def style_products(layers):
                for n in layers:
                    for c in range(KC):
                        k = (2 * n + c) * B
                        last = mm(psum[:, SUM_BANK[layers[0] > 0], k:k + B], aff_t[:, n, c * P:(c + 1) * P], cond_t[:, 0:B],
                                  start=True, stop=True)
                last.then_inc(su_style, 1)

            def square_sums(layers):
                for n in layers:
                    for o in range(KC):
                        k = 96 + (2 * n + o) * B
                        for c in range(KC):
                            last = mm(psum[:, SUM_BANK[layers[0] > 0], k:k + B], w_sq[:, n, c, o * P:(o + 1) * P], style2[:, 2 * n + c, :],
                                      start=(c == 0), stop=(c == KC - 1))
                last.then_inc(su_dem, 1)

            def x_transposes(a):
                pe.wait_ge(ld_x[a.par], 16 * (a.uses + 1))
                wait(pe, keys_ev, 4 * a.i)
                for c in range(KC):
                    for q in range(Q):
                        last = nc.tensor.transpose(pa[:, c, q * P:(q + 1) * P],
                                                   x_in[:, a.par, q, c * P:(c + 1) * P], ident[:, :])
                    last.then_inc(xt_mm, 1)

            def project_keys(a):
                pe.wait_ge(xt_ev, a.i + 1)
                pe.wait_ge(wk_done, 4 * (a.i + 1))
                for o in range(KC):
                    for b in range(NB):
                        for c in range(KC):
                            last = mm(pa[:, o, N * b:N * (b + 1)], w_mod[0][:, b, c, o * P:(o + 1) * P],
                                      x_t[:, c, N * b:N * (b + 1)], start=(c == 0), stop=(c == KC - 1))
                    last.then_inc(k_mm, 1)

            def decoder(half):
                for k in range(UCH // 2 * half, UCH // 2 * (half + 1)):
                    q = k % 4
                    w = min(512, NDEC - 512 * k)
                    mm(psum[32 * q:32 * q + 32, 6 + k // 4 % 2, 0:w], cond_t[:, :], w_dec_sb[:, 512 * k:512 * k + w],
                       start=True, stop=True).then_inc(su_u, 1)

            def scores(s, n):
                if n == 0:
                    pe.wait_ge(ld_gram[s.par], 16 * PLACED * (s.uses + 1))
                if isinstance(s.i, int) and s.i == 0 and n == 0:
                    pe.wait_ge(ld_mask[0], 32)
                wait(pe, z_done, CH * s.i + n - 1)
                left, right = (gram[0:98, s.par, side].rearrange("p h (t m) -> p (h t) m", t=2) for side in range(2))
                for g in range(GC):
                    grp = (g // 4) * GC + n * 4 + g % 4
                    for q in range(4):
                        last = mm(psum[32 * q:32 * q + 32, SC + n % 2, 32 * g:32 * g + 32],
                                  left[:, :, q * G + grp], right[:, :, q * G + grp],
                                  start=True, stop=True)
                last.then_inc(g_mm, 1)

            def values(s, n):
                if n == 0:
                    pe.wait_ge(ld_keys[s.par], 16 * (s.uses + 1))
                    if isinstance(s.i, int) and s.i == 0:
                        pe.wait_ge(su_o0, 1)
                k = CH * s.i + n
                pe.wait_ge(diag_done, 4 * (k + 1))
                wait(pe, o_ev, k - 1)
                for r in range(4):
                    for c in range(4):
                        last = mm(psum[32 * c:32 * c + D, OB + n % 2, P * r:P * (r + 1)],
                                  keys_v[:, s.par, :, c * GC + n * 4 + r], diag[:, n % 2, c * 4 + r, :],
                                  start=True, stop=True)
                last.then_inc(av_mm, 1)

            def project_o(c):
                pe.wait_ge(ld_o, 64 * (c.i + 1))
                pe.wait_ge(wo_done, c.i + 1)
                if isinstance(c.i, int) and c.i == STEPS - 1:
                    pe.wait_ge(keys_ev, 4 * STEPS)
                else:
                    wait(pe, out_ev, 2 * c.i)
                for o in range(KC):
                    for b in range(NB):
                        for k in range(KC):
                            src = o_t[:, k, :, 4 * b:4 * b + 4, :].rearrange("p c x g -> p x c g")
                            last = mm(rest_banks(c)[:, o, N * b:N * (b + 1)], w_mod[1][:, b, k, o * P:(o + 1) * P], src,
                                      start=(k == 0), stop=(k == KC - 1))
                    last.then_inc(c1_mm, 1)

            def layer1(c):
                pe.wait_ge(x1_done, 2 * (c.i + 1))
                pe.wait_ge(w1_done, c.i + 1)
                for o in range(KC):
                    for b in range(NB):
                        for k in range(KC):
                            last = mm(rest_banks(c)[:, o, N * b:N * (b + 1)], w_mod[2][:, b, k, o * P:(o + 1) * P],
                                      x1[:, k, N * b:N * (b + 1)], start=(k == 0), stop=(k == KC - 1))
                    last.then_inc(c2_mm, 1)

            def low_rank_in(c, w, src, done):
                for k in range(KC):
                    for b in range(NB):
                        last = mm(rest_banks(c)[64 * b:64 * b + 64, 0, 0:N], w[:, b, k, :], src[:, k, N * b:N * (b + 1)],
                                  start=(k == 0), stop=(k == KC - 1))
                last.then_inc(done, 1)

            def low_rank_out(c, w, src, done):
                for o in range(KC):
                    for b in range(NB):
                        last = mm(rest_banks(c)[:, o, N * b:N * (b + 1)], w[:, b, o * P:(o + 1) * P], src[:, :],
                                  start=True, stop=True)
                    last.then_inc(done, 1)

            def body(s, stages):
                c, a = preceding(s), following(s)
                attention, rest = "B" in stages, "C" in stages
                if "K" in stages:
                    project_keys(a)
                ends = isinstance(s.i, int) and s.i == STEPS - 1
                if ends:
                    scores(s, 2)
                    scores(s, 3)
                if rest and not (isinstance(s.i, int) and s.i == STEPS):
                    project_o(c)
                if attention and not ends:
                    scores(s, 2)
                    scores(s, 3)
                if ends:
                    values(s, 0)
                    values(s, 1)
                if rest:
                    layer1(c)
                if attention and not ends:
                    values(s, 0)
                    values(s, 1)
                if ends:
                    values(s, 2)
                if "X" in stages:
                    x_transposes(following(a))
                if rest:
                    pe.wait_ge(x2_done, 2 * (c.i + 1))
                    pe.wait_ge(gate_mul, 2 * (c.i + 1))
                    low_rank_in(c, w_down, x2, c3_mm)
                if attention:
                    values(s, 3 if ends else 2)
                if rest:
                    pe.wait_ge(act_done, c.i + 1)
                    low_rank_out(c, w_up_pad, act2, c4_mm)
                if attention and not ends:
                    values(s, 3)
                if rest:
                    pe.wait_ge(x3_done, 2 * (c.i + 1))
                    pe.wait_ge(u_done, 2 * (c.i + 1))
                    low_rank_in(c, u_pad, x3, c5_mm)
                if isinstance(s.i, int) and s.i == 0:
                    pe.wait_ge(ld_mask[1], 32)
                if "S" in stages:
                    scores(a, 0)
                if rest:
                    pe.wait_ge(y3_done, c.i + 1)
                    low_rank_out(c, v_pad, y3, c6_mm)
                if "S" in stages:
                    scores(a, 1)
                if ends:
                    project_o(s)
                if rest:
                    pe.wait_ge(x4_done, 2 * (c.i + 1))
                    for o in range(2):
                        for q in range(2 * o, 2 * o + 2):
                            for k in range(KC):
                                at = (q % 2) * F + k * P
                                last = nc.tensor.transpose(rest_banks(c)[:, o, at:at + P], x3[:, k, q * P:(q + 1) * P],
                                                           ident[:, :])
                        last.then_inc(c7_mm, 1)

            first = Step(0, 0, 0)
            pe.wait_ge(ident_1, 1)
            pe.wait_ge(ld_k, 16 * 4)
            affine_transposes(0)
            nc.tensor.transpose(psum[:, 1, F:F + B], raw_c[0:B, :], ident[0:B, 0:B]).then_inc(su_t, 1)
            weight_transposes(0)
            x_transposes(first)
            pe.wait_ge(su_aff, 2)
            style_products((0,))
            pe.wait_ge(su_st, 2)
            pe.wait_ge(su_sq, 1)
            square_sums((0,))
            project_keys(first)
            pe.wait_ge(ld_wdec, 16)
            pe.wait_ge(su_var, 1)
            decoder(0)
            x_transposes(following(first))
            pe.wait_ge(ld_w, 16 * 4)
            affine_transposes(1)
            affine_transposes(2).then_inc(su_t, 1)
            pe.wait_ge(su_perm, 2)
            weight_transposes(1)
            weight_transposes(2)
            pe.wait_ge(su_u_ev, 1)
            decoder(1)
            pe.wait_ge(su_aff, 4)
            style_products((1, 2))
            pe.wait_ge(ld_g, 16 * 5)
            mm(psum[0:32, 0, :], cond_t[:, :], gamma_beta[:, 2 * HID:640], start=True, stop=True)
            pe.wait_ge(su_ev, 2)
            pe.wait_ge(su_sq, 2)
            mm(psum[0:32, 3, 0:2 * HID], cond_t[:, :], gamma_beta[:, 0:2 * HID], start=True, stop=True)\
                .then_inc(su_rows, 1)
            pe.wait_ge(su_st, 5)
            pe.wait_ge(su_sq, LAYERS)
            square_sums((1, 2))
            project_keys(following(first))
            pe.wait_ge(su_rows_ev, 2)
            pe.wait_ge(su_var, 2)
            scores(first, 0)
            scores(first, 1)
            steps(pe, body)


_INS = ['x', 'cond_512', 'L0_cond_k_aff_w', 'L0_cond_k_aff_b', 'L0_cond_k_w', 'L0_cond_k_b', 'L0_cond_o_aff_w',
        'L0_cond_o_aff_b', 'L0_cond_o_w', 'L0_cond_o_b', 'L1_cond_weight', 'L1_cond_bias', 'L1_cond_affine_w',
        'L1_cond_affine_b', 'L2_cond_down_project', 'L2_cond_down_gamma', 'L2_cond_down_beta',
        'L2_cond_up_project', 'L2_cond_up_gamma', 'L2_cond_up_beta', 'L3_cond_W_dec', 'L3_cond_b_dec', 'L3_cond_V']
_OUTS = [((16, 256, 256), 'float32')]


def kernel(**inputs):
    import numpy as _np
    import concourse.bacc as _bacc
    from concourse import mybir as _mybir
    from concourse.bass_utils import run_bass_kernel_spmd as _run

    nc = _bacc.Bacc("TRN2", target_bir_lowering=False, num_devices=1)
    arrays, args = {}, []
    for name in _INS:
        a = _np.ascontiguousarray(inputs[name])
        arrays[f"in_{name}_dram"] = a
        args.append(nc.dram_tensor(f"in_{name}_dram", a.shape, _mybir.dt.from_np(a.dtype), kind="ExternalInput").ap())
    for i, (shape, dtype) in enumerate(_OUTS):
        dt = _mybir.dt.from_np(_np.dtype(dtype))
        args.append(nc.dram_tensor(f"out_{i}_dram", shape, dt, kind="ExternalOutput").ap())
    cond_resid_kernel(nc, *args)
    r = _run(nc, [arrays], core_ids=[0])
    got = tuple(r.results[0][f"out_{i}_dram"] for i in range(len(_OUTS)))
    return got[0]
```
